# Optimizing a Trainium2 kernel written in Bass

```python
import numpy as np
import jax
import jax.numpy as jnp

def _softmax(x, axis=-1):
    return jax.nn.softmax(x, axis=axis)

def _gelu(x):
    return jax.nn.gelu(x, approximate=True)

def _silu(x):
    return jax.nn.silu(x)

def _sigmoid(x):
    return jax.nn.sigmoid(x)

def _layernorm(x, axis=-1, eps=1e-05):
    m = jnp.mean(x, axis=axis, keepdims=True)
    v = jnp.var(x, axis=axis, keepdims=True)
    return (x - m) / jnp.sqrt(v + eps)

def _scatter_add(tgt, idx, src, axis=0):
    return tgt.at[idx].add(src)

def _segment_sum(src, seg, n):
    return jax.ops.segment_sum(src, seg, n)
kernel_name = 'mk_audio_tower_d1_tok_audfeat1024_r4_6a0ce5'

def setup_inputs(seed: int=0):
    np.random.seed(seed)
    _w = jnp.asarray

    def _rec_inputs():
        import jax
        import jax.numpy as jnp
        _rk = jax.random.key(seed)
        x = -7.10856e-05 + 0.999911 * jax.random.normal(jax.random.fold_in(_rk, 1), (64, 750, 256), jnp.float32)
        return x
    x = _rec_inputs()

    def _L0_tok_setup():
        import jax, jax.numpy as jnp
        import numpy as np
        BLOCK_SIZE = 16
        DIM = 256
        LN_EPS = 1e-05
        VAR_EPS = 1e-08
        key = jax.random.key(seed)
        ks = jax.random.split(key, 4)
        B, N, D = (8, 2048, DIM)
        x = jax.random.normal(ks[0], (B, N, D), dtype=jnp.float32)
        w_proj_w = jax.random.normal(ks[1], (D, 1), dtype=jnp.float32) * (1.0 / np.sqrt(D))
        w_proj_b = jnp.zeros((1,), dtype=jnp.float32)
        s_proj_w = jax.random.normal(ks[2], (3 * D, D), dtype=jnp.float32) * (1.0 / np.sqrt(3 * D))
        s_proj_b = jnp.zeros((D,), dtype=jnp.float32)
        ln_g = jnp.ones((D,), dtype=jnp.float32)
        ln_b = jnp.zeros((D,), dtype=jnp.float32)
        pos_emb = jax.random.normal(ks[3], (4096, D), dtype=jnp.float32)
        return {'x': x, 'w_proj_w': w_proj_w, 'w_proj_b': w_proj_b, 's_proj_w': s_proj_w, 's_proj_b': s_proj_b, 'ln_g': ln_g, 'ln_b': ln_b, 'pos_emb': pos_emb}
    _L0_tok_all = _L0_tok_setup()
    _L0_tok_in = {k: v for k, v in _L0_tok_all.items() if k in ('w_proj_w', 'w_proj_b', 's_proj_w', 's_proj_b', 'ln_g', 'ln_b', 'pos_emb')}
    del _L0_tok_all

    def _L0_attn_setup():
        import jax, jax.numpy as jnp
        import numpy as np
        HIDDEN, HEADS, HDIM = (256, 8, 64)
        B, S = (4, 2048)
        LN_EPS = 1e-06
        key = jax.random.key(seed)
        ks = jax.random.split(key, 12)
        inner = HEADS * HDIM
        sd = HIDDEN ** (-0.5)
        return {'x': jax.random.normal(ks[0], (B, S, HIDDEN), jnp.float32), 'Wq': jax.random.normal(ks[1], (HIDDEN, inner), jnp.float32) * sd, 'bq': jnp.zeros((inner,), jnp.float32), 'Wk': jax.random.normal(ks[2], (HIDDEN, inner), jnp.float32) * sd, 'bk': jnp.zeros((inner,), jnp.float32), 'Wv': jax.random.normal(ks[3], (HIDDEN, inner), jnp.float32) * sd, 'bv': jnp.zeros((inner,), jnp.float32), 'Wo': jax.random.normal(ks[4], (inner, HIDDEN), jnp.float32) * inner ** (-0.5), 'bo': jnp.zeros((HIDDEN,), jnp.float32), 'alpha': jnp.ones((HEADS, HDIM), jnp.float32), 'aug_param': jax.random.normal(ks[5], (1, HEADS, HDIM), jnp.float32), 'ln_scale': jnp.ones((HIDDEN,), jnp.float32), 'ln_bias': jnp.zeros((HIDDEN,), jnp.float32)}
    _L0_attn_all = _L0_attn_setup()
    _L0_attn_in = {k: v for k, v in _L0_attn_all.items() if k in ('Wq', 'bq', 'Wk', 'bk', 'Wv', 'bv', 'Wo', 'bo', 'alpha', 'aug_param', 'ln_scale', 'ln_bias')}
    del _L0_attn_all

    def _L0_ffn_setup():
        import jax, jax.numpy as jnp
        import numpy as np
        E = 8
        G = 4
        LG = 2
        TOPK = 2
        ROUTE_SCALE = 1.0

        def _grouped_mm(x, w, counts):
            counts = counts.astype(jnp.int32)
            if hasattr(jax.lax, 'ragged_dot'):
                return jax.lax.ragged_dot(x, w, counts)
            offs = jnp.cumsum(counts)
            eid = jnp.searchsorted(offs, jnp.arange(x.shape[0]), side='right')
            oh = jax.nn.one_hot(eid, w.shape[0], dtype=x.dtype)
            return jnp.einsum('nd,ne,edh->nh', x, oh, w)
        key = jax.random.key(seed)
        ks = jax.random.split(key, 8)
        bs, slen, dim, hid, shid = (2, 512, 256, 128, 256)
        std = 0.02
        return {'x': jax.random.normal(ks[0], (bs, slen, dim), jnp.float32), 'w_gate': jax.random.normal(ks[1], (E, dim), jnp.float32) * std, 'w1': jax.random.normal(ks[2], (E, dim, hid), jnp.float32) * std, 'w2': jax.random.normal(ks[3], (E, hid, dim), jnp.float32) * std, 'w3': jax.random.normal(ks[4], (E, dim, hid), jnp.float32) * std, 'sw1': jax.random.normal(ks[5], (shid, dim), jnp.float32) * std, 'sw2': jax.random.normal(ks[6], (dim, shid), jnp.float32) * std, 'sw3': jax.random.normal(ks[7], (shid, dim), jnp.float32) * std, 'expert_bias': jnp.zeros((E,), jnp.float32)}
    _L0_ffn_all = _L0_ffn_setup()
    _L0_ffn_in = {k: v for k, v in _L0_ffn_all.items() if k in ('w_gate', 'w1', 'w2', 'w3', 'sw1', 'sw2', 'sw3', 'expert_bias')}
    del _L0_ffn_all
    return {'x': x, 'L0_tok_w_proj_w': _L0_tok_in['w_proj_w'], 'L0_tok_w_proj_b': _L0_tok_in['w_proj_b'], 'L0_tok_s_proj_w': _L0_tok_in['s_proj_w'], 'L0_tok_s_proj_b': _L0_tok_in['s_proj_b'], 'L0_tok_ln_g': _L0_tok_in['ln_g'], 'L0_tok_ln_b': _L0_tok_in['ln_b'], 'L0_tok_pos_emb': _L0_tok_in['pos_emb'], 'L0_attn_Wq': _L0_attn_in['Wq'], 'L0_attn_bq': _L0_attn_in['bq'], 'L0_attn_Wk': _L0_attn_in['Wk'], 'L0_attn_bk': _L0_attn_in['bk'], 'L0_attn_Wv': _L0_attn_in['Wv'], 'L0_attn_bv': _L0_attn_in['bv'], 'L0_attn_Wo': _L0_attn_in['Wo'], 'L0_attn_bo': _L0_attn_in['bo'], 'L0_attn_alpha': _L0_attn_in['alpha'], 'L0_attn_aug_param': _L0_attn_in['aug_param'], 'L0_attn_ln_scale': _L0_attn_in['ln_scale'], 'L0_attn_ln_bias': _L0_attn_in['ln_bias'], 'L0_ffn_w_gate': _L0_ffn_in['w_gate'], 'L0_ffn_w1': _L0_ffn_in['w1'], 'L0_ffn_w2': _L0_ffn_in['w2'], 'L0_ffn_w3': _L0_ffn_in['w3'], 'L0_ffn_sw1': _L0_ffn_in['sw1'], 'L0_ffn_sw2': _L0_ffn_in['sw2'], 'L0_ffn_sw3': _L0_ffn_in['sw3'], 'L0_ffn_expert_bias': _L0_ffn_in['expert_bias']}

def reference(x, L0_tok_w_proj_w, L0_tok_w_proj_b, L0_tok_s_proj_w, L0_tok_s_proj_b, L0_tok_ln_g, L0_tok_ln_b, L0_tok_pos_emb, L0_attn_Wq, L0_attn_bq, L0_attn_Wk, L0_attn_bk, L0_attn_Wv, L0_attn_bv, L0_attn_Wo, L0_attn_bo, L0_attn_alpha, L0_attn_aug_param, L0_attn_ln_scale, L0_attn_ln_bias, L0_ffn_w_gate, L0_ffn_w1, L0_ffn_w2, L0_ffn_w3, L0_ffn_sw1, L0_ffn_sw2, L0_ffn_sw3, L0_ffn_expert_bias):
    import jax
    import jax.numpy as jnp

    def _L0_tok_ref(x, w_proj_w, w_proj_b, s_proj_w, s_proj_b, ln_g, ln_b, pos_emb):
        import jax, jax.numpy as jnp
        import numpy as np
        BLOCK_SIZE = 16
        DIM = 256
        LN_EPS = 1e-05
        VAR_EPS = 1e-08
        B, N, D = x.shape
        bs = BLOCK_SIZE
        pad = (bs - N % bs) % bs
        if pad > 0:
            x = jnp.pad(x, ((0, 0), (0, pad), (0, 0)))
        n_blocks = x.shape[1] // bs
        blocks = x.reshape(B, n_blocks, bs, D)
        w = jnp.einsum('bnkd,do->bnko', blocks, w_proj_w)[..., 0] + w_proj_b[0]
        w = jax.nn.softmax(w, axis=-1)
        wmean = jnp.einsum('bnk,bnkd->bnd', w, blocks)
        diff = blocks - wmean[:, :, None, :]
        wvar = jnp.einsum('bnk,bnkd->bnd', w, diff * diff)
        wstd = jnp.sqrt(wvar + VAR_EPS)
        bmax = blocks.max(axis=2)
        stats = jnp.concatenate([wmean, wstd, bmax], axis=-1)
        out = jnp.einsum('bnf,fd->bnd', stats, s_proj_w) + s_proj_b
        mu = out.mean(axis=-1, keepdims=True)
        var = out.var(axis=-1, keepdims=True)
        out = (out - mu) * jax.lax.rsqrt(var + LN_EPS) * ln_g + ln_b
        out = out + pos_emb[jnp.arange(n_blocks)]
        return out

    def _L0_attn_ref(x, Wq, bq, Wk, bk, Wv, bv, Wo, bo, alpha, aug_param, ln_scale, ln_bias):
        import jax, jax.numpy as jnp
        import numpy as np
        HIDDEN, HEADS, HDIM = (256, 8, 64)
        B, S = (4, 2048)
        LN_EPS = 1e-06
        b, s, _ = x.shape
        h, d = alpha.shape
        scale = d ** (-0.5)
        q = (x @ Wq + bq).reshape(b, s, h, d)
        k = (x @ Wk + bk).reshape(b, s, h, d)
        v = (x @ Wv + bv).reshape(b, s, h, d)
        decay = jax.nn.sigmoid(alpha)

        def step(state, qkv):
            q_t, k_t, v_t = qkv
            attn = jax.nn.softmax(jnp.einsum('bhd,bhd->bh', q_t, k_t) * scale, axis=-1)
            new_state = decay * state + (1.0 - decay) * attn[..., None] * v_t
            return (new_state, new_state)
        qs = jnp.moveaxis(q, 1, 0)
        ks_ = jnp.moveaxis(k, 1, 0)
        vs = jnp.moveaxis(v, 1, 0)
        init = jnp.zeros((b, h, d), x.dtype)
        _, states = jax.lax.scan(step, init, (qs, ks_, vs))
        states = jnp.moveaxis(states, 0, 1)
        aug = jax.nn.sigmoid(q * aug_param)
        out = (q * states + aug).reshape(b, s, h * d)
        out = out @ Wo + bo
        mean = jnp.mean(out, axis=-1, keepdims=True)
        var = jnp.var(out, axis=-1, keepdims=True)
        return (out - mean) * jax.lax.rsqrt(var + LN_EPS) * ln_scale + ln_bias

    def _L0_ffn_ref(x, w_gate, w1, w2, w3, sw1, sw2, sw3, expert_bias):
        import jax, jax.numpy as jnp
        import numpy as np
        E = 8
        G = 4
        LG = 2
        TOPK = 2
        ROUTE_SCALE = 1.0

        def _grouped_mm(x, w, counts):
            counts = counts.astype(jnp.int32)
            if hasattr(jax.lax, 'ragged_dot'):
                return jax.lax.ragged_dot(x, w, counts)
            offs = jnp.cumsum(counts)
            eid = jnp.searchsorted(offs, jnp.arange(x.shape[0]), side='right')
            oh = jax.nn.one_hot(eid, w.shape[0], dtype=x.dtype)
            return jnp.einsum('nd,ne,edh->nh', x, oh, w)
        bs, slen, dim = x.shape
        xf = x.reshape(-1, dim)
        N = xf.shape[0]
        logits = xf @ w_gate.T
        scores = jax.nn.softmax(logits.astype(jnp.float32), axis=-1)
        original = scores
        s = (scores + expert_bias).reshape(N, G, E // G)
        group_scores = jax.lax.top_k(s, 2)[0].sum(-1)
        top_groups = jax.lax.top_k(group_scores, LG)[1]
        keep = jnp.zeros((N, G), bool).at[jnp.arange(N)[:, None], top_groups].set(True)
        masked = jnp.where(keep[:, :, None], s, -jnp.inf).reshape(N, E)
        topk_idx = jax.lax.top_k(masked, TOPK)[1]
        weights = (jnp.take_along_axis(original, topk_idx, axis=1) * ROUTE_SCALE).astype(x.dtype)
        counts = jnp.bincount(topk_idx.reshape(-1), length=E)
        flat_idx = topk_idx.reshape(-1)
        routed_in = xf[flat_idx]
        routed_in = (routed_in.astype(jnp.float32) * weights.reshape(-1, 1)).astype(x.dtype)
        h = jax.nn.silu(_grouped_mm(routed_in, w1, counts)) * _grouped_mm(routed_in, w3, counts)
        routed_out = _grouped_mm(h, w2, counts)
        shared = jax.nn.silu(xf @ sw1.T) * (xf @ sw3.T) @ sw2.T
        out = shared.at[flat_idx].add(routed_out)
        return out.reshape(bs, slen, dim)
    h = _L0_tok_ref(x, L0_tok_w_proj_w, L0_tok_w_proj_b, L0_tok_s_proj_w, L0_tok_s_proj_b, L0_tok_ln_g, L0_tok_ln_b, L0_tok_pos_emb)
    h = h + _L0_attn_ref(_layernorm(h, axis=-1), L0_attn_Wq, L0_attn_bq, L0_attn_Wk, L0_attn_bk, L0_attn_Wv, L0_attn_bv, L0_attn_Wo, L0_attn_bo, L0_attn_alpha, L0_attn_aug_param, L0_attn_ln_scale, L0_attn_ln_bias)
    h = h + _L0_ffn_ref(_layernorm(h, axis=-1), L0_ffn_w_gate, L0_ffn_w1, L0_ffn_w2, L0_ffn_w3, L0_ffn_sw1, L0_ffn_sw2, L0_ffn_sw3, L0_ffn_expert_bias)
    return h

_drawn_inputs = setup_inputs


def setup_inputs(seed=0):
    import zlib

    import numpy as np

    out = dict(_drawn_inputs(seed))
    spreads = {'L0_tok_s_proj_b': (0.0, 0.1),
     'L0_tok_ln_g': (1.0, 0.2),
     'L0_tok_ln_b': (0.0, 0.1),
     'L0_attn_bq': (0.0, 0.344),
     'L0_attn_bk': (0.0, 0.8),
     'L0_attn_bv': (0.0, 0.6),
     'L0_attn_bo': (0.0, 0.1),
     'L0_attn_alpha': (1.0, 0.6),
     'L0_attn_ln_scale': (1.0, 0.2),
     'L0_attn_ln_bias': (0.0, 0.1),
     'L0_ffn_expert_bias': (0.0, 0.8)}
    factors = {'L0_ffn_w_gate': 8.0,
     'L0_ffn_w1': 8.0,
     'L0_ffn_w2': 8.0,
     'L0_ffn_w3': 8.0,
     'L0_ffn_sw1': 6.238,
     'L0_ffn_sw2': 6.19,
     'L0_ffn_sw3': 5.86}
    for name, (base, spread) in spreads.items():
        noise = np.random.default_rng([zlib.crc32(name.encode()), seed]).standard_normal(out[name].shape)
        drawn = base * np.exp(spread * noise) if base else spread * noise
        out[name] = jnp.asarray(drawn.astype(out[name].dtype))
    for name, factor in factors.items():
        out[name] = (out[name] * factor).astype(out[name].dtype)
    return out
```

```python
from contextlib import ExitStack

import numpy as np

import concourse.bass as bass
from concourse import mybir

F32 = mybir.dt.float32
ALU = mybir.AluOpType
ACT = mybir.ActivationFunctionType
AX = mybir.AxisListType

P = 128
CLIPS, ROWS, D = 64, 750, 256
BLOCK = 16
NBLK = -(-ROWS // BLOCK)
TILES = -(-NBLK // 2)
ST = 4
JR = 4
Q = BLOCK // JR
BL = P // Q
HEADS, HD = 8, 64
CH = HEADS * HD
NC = CH // P
E, HID = 8, 128
G = 4
PAIRS = E * E
POS_ROWS = NBLK + 1
LN_TOK, LN_ATT, LN_H, VAR_EPS = 1e-5, 1e-6, 1e-5, 1e-8

C_ID, C_ONES, C_BLK, C_MASK, C_HALF = 0, 128, 256, 384, 416
C_EPS = C_HALF + 1
C_POS = C_EPS + 4
C_LT8 = C_POS + 2 * TILES
C_LT4 = C_LT8 + 64
C_END = C_LT4 + 16


def constants():
    p = np.arange(P)
    c = np.zeros((P, C_END), np.float32)
    c[:, C_ID:C_ID + P] = np.eye(P)
    c[:, C_ONES:C_ONES + P] = 1.0
    c[:, C_BLK:C_BLK + P] = p[:, None] // Q == p[None, :] // Q
    c[:, C_MASK:C_MASK + BL] = p[:, None] // Q == np.arange(BL)[None, :]
    c[:, C_HALF] = -0.5
    c[:, C_EPS:C_EPS + 4] = (LN_TOK, LN_H, LN_ATT, LN_H)
    t = np.arange(TILES)[None, :, None]
    s = np.arange(2)[None, None, :]
    token = (p[:, None, None] % CLIPS) * NBLK + 2 * t + p[:, None, None] // CLIPS
    c[:, C_POS:C_POS + 2 * TILES] = (2 * token + s).reshape(P, -1)
    c[:, C_LT8:C_LT8 + 64] = (np.arange(8)[None, :] < np.arange(8)[:, None]).reshape(-1)
    c[:, C_LT4:C_LT4 + 16] = (np.arange(4)[None, :] < np.arange(4)[:, None]).reshape(-1)
    return c


def audio_tower(nc, a, out):
    x = a["x"]
    with ExitStack() as ctx:
        def sb(name, *shape):
            return ctx.enter_context(nc.sbuf_tensor(name, list(shape), F32))

        def sem(name):
            return ctx.enter_context(nc.semaphore(name))

        const = sb("const", P, C_END)
        ident = const[:, C_ID:C_ID + P]
        ones = const[:, C_ONES:C_ONES + P]
        same_block = const[:, C_BLK:C_BLK + P]
        block_mask = const[:, C_MASK:C_MASK + BL]
        minus_half = const[:, C_HALF:C_HALF + 1]
        wproj = sb("wproj", P, D)
        wproj_b = sb("wproj_b", P, 1)
        sproj = sb("sproj", P, 6, D)
        wq, wk, wv = sb("wq", P, 2, CH), sb("wk", P, 2, CH), sb("wv", P, 2, CH)
        wo = sb("wo", P, NC, D)
        gate_up1 = sb("gate_up1", P, 2, E + D)
        up3 = sb("up3", P, 2, D)
        down = sb("down", P, 2, D)
        w1, w3 = sb("w1", P, 2, E, HID), sb("w3", P, 2, E, HID)
        w2 = sb("w2", HID, E, D)
        sproj_b, ln_g, ln_b = sb("sproj_b", P, D), sb("ln_g", P, D), sb("ln_b", P, D)
        bq, bk, bv = sb("bq", P, CH), sb("bk", P, CH), sb("bv", P, CH)
        bo, att_g, att_b = sb("bo", P, D), sb("att_g", P, D), sb("att_b", P, D)
        ebias = sb("ebias", P, E)
        alpha_cols, aug_cols = sb("alpha_cols", P, NC), sb("aug_cols", P, NC)
        decay_cols = sb("decay_cols", P, NC)
        keep_row = sb("keep_row", P, CH)
        zeros = a["zeros"]

        xx = [sb(f"xx{i}", P, 2, ST * JR * D) for i in range(2)]
        product = sb("product", P, JR, D)
        max2, max1 = sb("max2", P, ST, 2 * D), sb("max1", P, ST, D)
        logit = sb("logit", P, ST * JR)
        logit_max, block_max, block_max4 = sb("logit_max", P, ST), sb("block_max", ST, BL), sb("block_max4", ST, BL, Q)
        shifted, expo, weight = sb("shifted", P, ST * JR), sb("expo", P, ST * JR), sb("weight", P, ST * JR)
        expo_sum, inv_sum = sb("expo_sum", P, ST), sb("inv_sum", P, ST)
        spread = sb("spread", P, ST, JR, BL)
        mean_var, mean_sq = sb("mean_var", P, 2, D), sb("mean_sq", P, D)
        stats = [sb(f"stats{i}", P, 6, P) for i in range(2)]
        pos = [sb(f"pos{i}", P, D) for i in range(2)]
        pos_b = sb("pos_b", P, D)
        h0, h0c = sb("h0", P, D), sb("h0c", P, D)
        bn = [sb(f"bn{i}", P, 6) for i in range(4)]
        mv = [sb(f"mv{i}", P, 2) for i in range(4)]
        ve = [sb(f"ve{i}", P, 1) for i in range(4)]
        rstd = [sb(f"rstd{i}", P, 1) for i in range(4)]
        h1 = [sb(f"h1_{i}", P, D) for i in range(2)]
        a_in, aT = sb("a_in", P, D), sb("aT", P, 2, P)
        qb, kb, vb, kq = sb("qb", P, CH), sb("kb", P, CH), sb("vb", P, CH), sb("kq", P, CH)
        score, neg_max, e_score = sb("score", P, HEADS), sb("neg_max", P, 1), sb("e_score", P, HEADS)
        s_sum, s_inv, attn = sb("s_sum", P, 1), sb("s_inv", P, 1), sb("attn", P, HEADS)
        u = sb("u", P, CH)
        aug = sb("aug", P, NC, P)
        state = [sb(f"state{i}", P, NC, P) for i in range(2)]
        qs = sb("qs", P, NC, P)
        oT = [sb(f"oT{i}", P, NC, P) for i in range(2)]
        h1b, o_raw, o_c, h2 = sb("h1b", P, D), sb("o_raw", P, D), sb("o_c", P, D), sb("h2", P, D)
        z, zT = sb("z", P, D), sb("zT", P, 2, P)
        z_first = sb("z_first", P, 2, 2 * TILES)
        gate = sb("gate", P, TILES, E)
        half_tanh, g1, g2, gT = sb("half_tanh", P, D), sb("g1", P, D), sb("g2", P, D), sb("gT", P, 2, P)
        h3 = [sb(f"h3_{i}", P, D) for i in range(2)]

        spares = [b[:].rearrange("p k n -> p (k n)") for b in xx]
        used = [0]

        def carve(name, *shape):
            size = int(np.prod(shape[1:]))
            if used[0] + size > 2 * ST * JR * D:
                spares.pop(0)
                used[0] = 0
            part = spares[0][0:shape[0], used[0]:used[0] + size]
            used[0] += size
            if len(shape) == 2:
                return part
            dims = " ".join("abc"[:len(shape) - 1])
            return part.rearrange(f"p ({dims}) -> p {dims}", **dict(zip("abc", shape[1:])))

        sc, s2, s3 = carve("sc", P, TILES, E), carve("s2", P, TILES, E), carve("s3", P, TILES, E)
        t1, gsum, grank = carve("t1", P, TILES), carve("gsum", P, TILES, G), carve("grank", P, TILES, G)
        cmp_gt, cmp_ge = carve("cmp_gt", P, TILES * E * E), carve("cmp_ge", P, TILES * E * E)
        rank = carve("rank", P, TILES, E)
        chosen, chosen_w, segment, seg_hi = (carve(n, P, 2 * TILES, E) for n in ("chosen", "chosen_w", "segment", "seg_hi"))
        slot_w = carve("slot_w", P, 2 * TILES)
        mine, count, seg_end, seg_start = (carve(n, P, E) for n in ("mine", "count", "seg_end", "seg_start"))
        tab_rows = carve("tab_rows", E, 2, E * HID)
        tab = carve("tab", P, 2, HID)
        pairs, pairs_w = ([carve(f"{n}{i}", P, 2, E, E) for i in range(2)] for n in ("pairs", "pairs_w"))
        pairs_wT = [carve(f"pairs_wT{i}", P, P) for i in range(2)]
        r_tanh, r1, r2 = ([carve(f"{n}{i}", P, 2, HID) for i in range(2)] for n in ("r_tanh", "r1_", "r2_"))
        hsum, hsumT0, hsumT = carve("hsum", P, HID), carve("hsumT0", P, PAIRS), carve("hsumT", P, PAIRS)
        first8, first8_out = carve("first8", E, D), carve("first8_out", E, D)

        psum = ctx.enter_context(nc.psum_tensor("psum", [P, 8, 512], F32))
        bank = [psum[:, i, :] for i in range(8)]

        weights_in = sem("weights_in")
        setup_act, setup_dve = sem("setup_act"), sem("setup_dve")
        x_in = [sem(f"x_in{i}") for i in range(2)]
        pos_in = [sem(f"pos_in{i}") for i in range(2)]
        stored = [sem(f"stored{i}") for i in range(2)]
        names = """dot0 dot1 dot2 dot3 maxed2 maxed1 squared lmaxed lmaxT bmaxed0 bmaxed bmaxT shifted exped esummed denned rdenned
            weighted spreaded summed maxT maxq meaned msqed varred varred2 statT statevac
            sprojed h0ed bn0 mv0 ve0 rstd0 posb h0ced h1ed bn1 mv1 ve1 rstd1 a_ined aTed aTevac qed ked ved
            qbed kbed vcopied vbed kqed scored nmaxed eed sinved attned ued qTed uTed tanhed auged
            stated0 stated1 qsed oTed
            woed h1bed oed bn2 mv2 ve2 rstd2 oced h2ed bn3 mv3 ve3 rstd3 zed zTed zTevac zfirst
            ffned3 ffned1 gated htanh g1ed g2ed gTed gTevac downed h3ed""".split()
        names += "tabbed tabrowed paired pairwed pairTed pairTevac looked rtanhed r1ed r2ed acced".split()
        route, gate_exp, counted, rouT, hsummed, hsumT_pe, hsumT_act, final_pe, final_dve = (
            sem(n) for n in "route gate_exp counted rouT hsummed hsumT_pe hsumT_act final_pe final_dve".split())
        last_in, tab_in, first8_in, first8_stored = (sem(n) for n in "last_in tab_in first8_in first8_stored".split())
        S = {n: sem("s_" + n) for n in names}

        def done(eng, name, tile, lag=0):
            value = tile[0] + 1 - lag
            if isinstance(value, int) and value < 1:
                return
            eng.wait_ge(S[name], value)

        block = ctx.enter_context(nc.Block())
        row_h = lambda ap: ap.rearrange("(a n) -> a n", a=1)
        weight_loads = [
            (const[:], a["const"]),
            (wproj[:], a["L0_tok_w_proj_w"].rearrange("d a -> a d").broadcast_to([P, D])),
            (wproj_b[:], row_h(a["L0_tok_w_proj_b"]).broadcast_to([P, 1])),
            (sproj[:], a["L0_tok_s_proj_w"].rearrange("(c p) n -> p c n", p=P)),
            (sproj_b[:], row_h(a["L0_tok_s_proj_b"]).broadcast_to([P, D])),
            (ln_g[:], row_h(a["L0_tok_ln_g"]).broadcast_to([P, D])),
            (ln_b[:], row_h(a["L0_tok_ln_b"]).broadcast_to([P, D])),
            (wq[:], a["L0_attn_Wq"].rearrange("(c p) n -> p c n", p=P)),
            (wk[:], a["L0_attn_Wk"].rearrange("(c p) n -> p c n", p=P)),
            (wv[:], a["L0_attn_Wv"].rearrange("(c p) n -> p c n", p=P)),
            (bq[:], row_h(a["L0_attn_bq"]).broadcast_to([P, CH])),
            (bk[:], row_h(a["L0_attn_bk"]).broadcast_to([P, CH])),
            (bv[:], row_h(a["L0_attn_bv"]).broadcast_to([P, CH])),
            (wo[:], a["L0_attn_Wo"].rearrange("(c p) n -> p c n", p=P)),
            (bo[:], row_h(a["L0_attn_bo"]).broadcast_to([P, D])),
            (att_g[:], row_h(a["L0_attn_ln_scale"]).broadcast_to([P, D])),
            (att_b[:], row_h(a["L0_attn_ln_bias"]).broadcast_to([P, D])),
            (keep_row[:], a["L0_attn_alpha"].rearrange("h d -> (h d)").rearrange("(a n) -> a n", a=1).broadcast_to([P, CH])),
            (alpha_cols[:], a["alpha_cols"]),
            (aug_cols[:], a["aug_cols"]),
            (gate_up1[:, :, 0:E], a["w_gate_T"].rearrange("(c p) n -> p c n", p=P)),
            (gate_up1[:, :, E:E + D], a["sw1_T"].rearrange("(c p) n -> p c n", p=P)),
            (up3[:], a["sw3_T"].rearrange("(c p) n -> p c n", p=P)),
            (down[:], a["sw2_T"].rearrange("(c p) n -> p c n", p=P)),
            (ebias[:], row_h(a["L0_ffn_expert_bias"]).broadcast_to([P, E])),
            (w1[:, 0], a["L0_ffn_w1"][:, 0:P, :].rearrange("e p n -> p e n")),
            (w1[:, 1], a["L0_ffn_w1"][:, P:2 * P, :].rearrange("e p n -> p e n")),
            (w3[:, 0], a["L0_ffn_w3"][:, 0:P, :].rearrange("e p n -> p e n")),
            (w3[:, 1], a["L0_ffn_w3"][:, P:2 * P, :].rearrange("e p n -> p e n")),
            (w2[:], a["L0_ffn_w2"].rearrange("e p n -> p e n")),
        ]
        ALL_WEIGHTS = 16 * len(weight_loads)

        def tile_of(h, c):
            return (2 * h + c, c % 2, h + c // 2)

        def periods(eng, period, between=None):
            tiles = lambda k: [tile_of(0, k - d) if 0 <= k - d < TILES else None for d in range(3)]
            for k in range(4):
                period(*tiles(k))
            with eng.Fori(2, TILES // 2) as h:
                for c in range(2):
                    period(tile_of(h, c), tile_of(h, c - 1), tile_of(h, c - 2))
            period(*tiles(TILES))
            if between:
                between()
            period(*tiles(TILES + 1))

        def routed_tiles(eng, routed):
            for t in range(2):
                routed(tile_of(0, t), t == 0)
            with eng.Fori(1, TILES // 2) as h:
                for c in range(2):
                    routed(tile_of(h, c), False)

        @block.sync
        def _(sp):
            def buffer_read(tile):
                for step in ("maxed2", "squared", "summed"):
                    done(sp, step, tile, 2)

            def load_x(tile):
                t, p, n = tile
                buffer_read(tile)
                for s in range(ST):
                    tl, bh = s // 2, s % 2
                    src = x[bh * BL:(bh + 1) * BL, bass.ds((2 * t + tl) * BLOCK, BLOCK), :]
                    sp.dma_start(xx[p][:, 0, s * JR * D:(s + 1) * JR * D],
                                 src.rearrange("b (q j) d -> b q (j d)", q=Q)).then_inc(x_in[p], 16)

            def load_last_x(tile):
                p = tile[1]
                start = (NBLK - 1) * BLOCK
                rows = ROWS - start - (Q - 1) * JR
                buffer_read(tile)
                for bh in range(2):
                    cols = xx[p][:, 0, bh * JR * D:(bh + 1) * JR * D]
                    for q in range(Q - 1):
                        sp.dma_start(cols[q:P:Q, :], x[bh * BL:(bh + 1) * BL, start + q * JR:start + (q + 1) * JR, :]
                                     .rearrange("b j d -> b (j d)")).then_inc(last_in, 16)
                    sp.dma_start(cols[Q - 1:P:Q, rows * D:], zeros[0:BL, rows * D:]).then_inc(last_in, 16)
                sp.wait_ge(last_in, 16 * 2 * Q)
                for bh in range(2):
                    sp.dma_start(xx[p][Q - 1:P:Q, 0, bh * JR * D:bh * JR * D + rows * D],
                                 x[bh * BL:(bh + 1) * BL, ROWS - rows:ROWS, :].rearrange("b j d -> b (j d)")).then_inc(x_in[p], 16)
                    sp.dma_start(xx[p][:, 0, (2 + bh) * JR * D:(3 + bh) * JR * D], zeros[:, :]).then_inc(x_in[p], 16)

            def load_pos(tile):
                t, p, n = tile
                done(sp, "posb", tile, 2)
                for tl in range(2):
                    sp.dma_start(pos[p][tl * CLIPS:(tl + 1) * CLIPS, :],
                                 a["L0_tok_pos_emb"][bass.ds(2 * t + tl, 1), :].broadcast_to([CLIPS, D])).then_inc(pos_in[p], 16)

            def store(tile, steps=2):
                t, p, n = tile
                done(sp, "h3ed", tile)
                for tl in range(steps):
                    sp.dma_start(out[:, bass.ds(2 * t + tl, 1), :].rearrange("b t d -> b (t d)"),
                                 h3[p][tl * CLIPS:(tl + 1) * CLIPS, :]).then_inc(stored[p], 16)

            load_x(tile_of(0, 0))
            for dst, src in weight_loads:
                sp.dma_start(dst, src).then_inc(weights_in, 16)
            load_x(tile_of(0, 1))
            for k in range(4):
                load_x(tile_of(0, k + 2))
                load_pos(tile_of(0, k))
                if k >= 2:
                    store(tile_of(0, k - 2))
            with sp.Fori(2, TILES // 2 - 2) as h:
                for c in range(2):
                    load_x(tile_of(h, c + 2))
                    load_pos(tile_of(h, c))
                    store(tile_of(h, c - 2))
            for k in range(TILES - 4, TILES + 2):
                if k + 2 == TILES - 1:
                    load_last_x(tile_of(0, k + 2))
                elif k + 2 < TILES:
                    load_x(tile_of(0, k + 2))
                if k < TILES:
                    load_pos(tile_of(0, k))
                if k == TILES:
                    done(sp, "tabrowed", tile_of(0, 0))
                    for s in range(2):
                        for kind in range(2):
                            sp.dma_start(tab[s * PAIRS:(s + 1) * PAIRS, kind, :],
                                         tab_rows[:, kind, :].rearrange("e (g n) -> e g n", g=E)).then_inc(tab_in, 16)
                store(tile_of(0, k - 2), 1 if k - 2 == TILES - 1 else 2)
            sp.wait_ge(stored[0], 32 * (TILES // 2))
            sp.wait_ge(stored[1], 32 * (TILES // 2) - 16)
            sp.dma_start(first8[:], out[0, 0:E, :]).then_inc(first8_in, 16)
            sp.wait_ge(final_dve, 1)
            sp.dma_start(out[0, 0:E, :], first8_out[:]).then_inc(first8_stored, 16)
            sp.wait_ge(first8_stored, 16)

        @block.gpsimd
        def _(pool):
            def rstd_of(i, tile):
                done(pool, f"mv{i}", tile)
                pool.tensor_tensor(ve[i][:], mv[i][:, 1:2], const[:, C_EPS + i:C_EPS + i + 1], ALU.add).then_inc(S[f"ve{i}"], 1)
                done(pool, f"ve{i}", tile)
                pool.tensor_tensor(rstd[i][:], ve[i][:], minus_half, ALU.pow).then_inc(S[f"rstd{i}"], 1)

            def spread_weights(tile):
                done(pool, "weighted", tile)
                done(pool, "summed", tile, 1)
                pool.tensor_tensor(spread[:].rearrange("p s j b -> p (s j) b"),
                                   weight[:].rearrange("p (c a) -> p c a", a=1).broadcast_to([P, ST * JR, BL]),
                                   block_mask.rearrange("p (a b) -> p a b", a=1).broadcast_to([P, ST * JR, BL]),
                                   ALU.mult).then_inc(S["spreaded"], 1)

            def add_pos(tile):
                t, p, n = tile
                pool.wait_ge(pos_in[p], 32 * (n + 1))
                done(pool, "h1ed", tile, 1)
                pool.tensor_tensor(pos_b[:], pos[p][:], ln_b[:], ALU.add).then_inc(S["posb"], 1)

            def key_query(tile):
                done(pool, "qbed", tile)
                done(pool, "kbed", tile)
                done(pool, "scored", tile, 1)
                pool.tensor_tensor(kq[:], qb[:], kb[:], ALU.mult).then_inc(S["kqed"], 1)

            def value_bias(tile):
                done(pool, "vcopied", tile)
                pool.tensor_tensor(vb[:], vb[:], bv[:], ALU.add).then_inc(S["vbed"], 1)

            def weigh_value(tile):
                done(pool, "attned", tile)
                done(pool, "vbed", tile)
                done(pool, "uTed", tile, 1)
                pool.tensor_tensor(u[:].rearrange("p (h d) -> p h d", h=HEADS), vb[:].rearrange("p (h d) -> p h d", h=HEADS),
                                   attn[:].rearrange("p (h a) -> p h a", a=1).broadcast_to([P, HEADS, HD]), ALU.mult).then_inc(S["ued"], 1)

            def add_aug(tile):
                done(pool, "qsed", tile)
                done(pool, "auged", tile)
                done(pool, "woed", tile, 2)
                pool.tensor_tensor(oT[tile[1]][:], qs[:], aug[:], ALU.add).then_inc(S["oTed"], 1)

            def residual_bias(tile):
                done(pool, "h1ed", tile)
                done(pool, "h2ed", tile, 1)
                pool.tensor_tensor(h1b[:], h1[tile[1]][:], att_b[:], ALU.add).then_inc(S["h1bed"], 1)

            def period(A, B, C):
                if C:
                    residual_bias(C)
                    rstd_of(2, C)
                if B:
                    add_pos(B)
                    rstd_of(0, B)
                if C:
                    rstd_of(3, C)
                if B:
                    rstd_of(1, B)
                if A:
                    spread_weights(A)
                if B:
                    key_query(B)
                    value_bias(B)
                    weigh_value(B)
                    add_aug(B)

            def routed(tile, first):
                t, p, n = tile
                done(pool, "acced", tile, 2)
                pool.tensor_tensor(pairs[p][:].rearrange("p s e g -> p s e g"),
                                   chosen[:, bass.ds(2 * t, 2), :].rearrange("p s (e a) -> p s e a", a=1).broadcast_to([P, 2, E, E]),
                                   segment[:, bass.ds(2 * t, 2), :].rearrange("p s (a g) -> p s a g", a=1).broadcast_to([P, 2, E, E]),
                                   ALU.mult).then_inc(S["paired"], 1)

            pool.wait_ge(weights_in, ALL_WEIGHTS)
            pool.wait_ge(setup_dve, 1)
            periods(pool, period)
            pool.wait_ge(route, ROUTE_DONE)
            routed_tiles(pool, routed)

        @block.scalar
        def _(act):
            def squares(tile):
                t, p, n = tile
                act.wait_ge(x_in[p], 64 * (n + 1))
                done(act, "summed", tile, 2)
                act.activation(xx[p][:, 1, :], xx[p][:, 0, :], ACT.Square).then_inc(S["squared"], 1)

            def exp_logits(tile):
                done(act, "shifted", tile)
                act.activation(expo[:], shifted[:], ACT.Exp).then_inc(S["exped"], 1)

            def mean_and_square(tile):
                done(act, "summed", tile)
                act.activation(mean_var[:, 0, :], bank[0][:, 0:D], ACT.Copy).then_inc(S["meaned"], 1)
                act.activation(mean_sq[:], bank[0][:, 0:D], ACT.Square).then_inc(S["msqed"], 1)

            def evacuate_stats(tile):
                p = tile[1]
                done(act, "statT", tile)
                done(act, "sprojed", tile, 2)
                act.activation(stats[p][:, 0:2, :].rearrange("p c n -> p (c n)"), bank[0][:, 0:2 * P], ACT.Copy)
                act.activation(stats[p][:, 2:4, :].rearrange("p c n -> p (c n)"), bank[0][:, 2 * P:4 * P], ACT.Sqrt).then_inc(S["statevac"], 1)

            def evacuate_a(tile):
                done(act, "aTed", tile)
                act.activation(aT[:].rearrange("p c n -> p (c n)"), bank[4][:, 0:D], ACT.Copy).then_inc(S["aTevac"], 1)

            def copy_value(tile):
                done(act, "ved", tile)
                done(act, "ued", tile, 1)
                act.activation(vb[:], bank[4][:, :], ACT.Copy).then_inc(S["vcopied"], 1)

            def exp_scores(tile):
                done(act, "nmaxed", tile)
                act.activation(e_score[:], score[:], ACT.Exp, bias=neg_max[:, 0:1], accum_out=s_sum[:, 0:1]).then_inc(S["eed"], 1)

            def augment(tile):
                done(act, "qTed", tile)
                done(act, "oTed", tile, 1)
                for c in range(NC):
                    last = act.activation(aug[:, c, :], bank[5][:, c * P:(c + 1) * P], ACT.Tanh, scale=aug_cols[:, c:c + 1])
                last.then_inc(S["tanhed"], 1)
                done(act, "tanhed", tile)
                act.activation(aug[:], aug[:], ACT.Copy, bias=0.5, scale=0.5).then_inc(S["auged"], 1)

            def evacuate_z(tile):
                t = tile[0]
                done(act, "zTed", tile)
                act.activation(zT[:].rearrange("p c n -> p (c n)"), bank[7][:, 0:D], ACT.Copy).then_inc(S["zTevac"], 1)
                act.activation(z_first[:, :, bass.ds(2 * t, 2)], bank[7][:, 0:D].rearrange("p (c n) -> p c n", c=2)[:, :, 0:P:CLIPS],
                               ACT.Copy).then_inc(S["zfirst"], 1)

            def gate_and_tanh(tile):
                t = tile[0]
                done(act, "ffned1", tile)
                act.activation(gate[:, bass.ds(t, 1), :].rearrange("p a e -> p (a e)"), bank[6][:, 0:E], ACT.Copy).then_inc(S["gated"], 1)
                done(act, "g1ed", tile, 1)
                act.activation(half_tanh[:], bank[6][:, E:E + D], ACT.Tanh, scale=0.5).then_inc(S["htanh"], 1)

            def evacuate_g(tile):
                done(act, "gTed", tile)
                act.activation(gT[:].rearrange("p c n -> p (c n)"), bank[6][:, 0:D], ACT.Copy).then_inc(S["gTevac"], 1)

            def period(A, B, C):
                if A:
                    squares(A)
                if C:
                    evacuate_z(C)
                if B:
                    evacuate_a(B)
                if A:
                    exp_logits(A)
                if C:
                    gate_and_tanh(C)
                    evacuate_g(C)
                if B:
                    copy_value(B)
                    augment(B)
                    exp_scores(B)
                if A:
                    mean_and_square(A)
                    evacuate_stats(A)

            def table_rows():
                done(act, "tabbed", tile_of(0, 0))
                for b in range(4):
                    last = act.activation(tab_rows[:, b // 2, (b % 2) * 512:(b % 2 + 1) * 512], bank[b][0:E, :], ACT.Copy)
                last.then_inc(S["tabrowed"], 1)

            def routed(tile, first):
                t, p, n = tile
                done(act, "pairTed", tile)
                done(act, "looked", tile, 2)
                act.activation(pairs_wT[p][:], bank[1 + p][:, 0:P], ACT.Copy).then_inc(S["pairTevac"], 1)
                done(act, "looked", tile)
                done(act, "r1ed", tile, 2)
                act.activation(r_tanh[p][:], psum[:, 4 + 2 * p:6 + 2 * p, 0:HID], ACT.Tanh, scale=0.5).then_inc(S["rtanhed"], 1)

            act.wait_ge(weights_in, ALL_WEIGHTS)
            act.activation(alpha_cols[:], alpha_cols[:], ACT.Tanh, scale=0.5).then_inc(setup_act, 1)
            act.activation(keep_row[:], keep_row[:], ACT.Tanh, scale=0.5).then_inc(setup_act, 1)
            act.wait_ge(setup_dve, 1)
            periods(act, period, table_rows)
            act.wait_ge(route, GATE_SHIFTED)
            act.activation(sc[:], sc[:], ACT.Exp).then_inc(gate_exp, 1)
            routed_tiles(act, routed)
            done(act, "acced", tile_of(0, TILES - 1))
            act.activation(hsum[:], bank[0][:, 0:HID], ACT.Copy).then_inc(hsummed, 1)
            act.wait_ge(hsumT_pe, 1)
            act.activation(hsumT0[:], bank[1][:, 0:PAIRS], ACT.Copy).then_inc(hsumT_act, 1)

        @block.tensor
        def _(pe):
            def logit_max_rows(tile):
                done(pe, "lmaxed", tile)
                pe.transpose(bank[1][0:ST, 0:P], logit_max[:], ident).then_inc(S["lmaxT"], 1)

            def block_max_cols(tile):
                done(pe, "bmaxed", tile)
                pe.matmul(bank[1][:, P:P + ST], block_max4[:].rearrange("s b q -> s (b q)"),
                          ident[0:ST, 0:ST], start=True, stop=True).then_inc(S["bmaxT"], 1)

            def block_sums(tile):
                done(pe, "esummed", tile)
                pe.matmul(bank[1][:, P:P + ST], same_block, expo_sum[:], start=True, stop=True).then_inc(S["denned"], 1)

            def weighted_sums(tile):
                p = tile[1]
                done(pe, "spreaded", tile)
                done(pe, "squared", tile)
                done(pe, "statevac", tile, 1)
                for j in range(JR):
                    for s in range(ST):
                        col = (s * JR + j) * D
                        last = pe.matmul(bank[0][s * BL:(s + 1) * BL, :], spread[:, s, j, :], xx[p][:, :, col:col + D],
                                         start=(j == 0), stop=(j == JR - 1), tile_position=(0, s * BL))
                last.then_inc(S["summed"], 1)

            def transpose_maxima(tile):
                done(pe, "maxed1", tile)
                done(pe, "maxq", tile, 1)
                for c in range(2):
                    for s in range(ST):
                        last = pe.transpose(bank[2 + c][:, s * P:(s + 1) * P], max1[:, s, c * P:(c + 1) * P], ident)
                last.then_inc(S["maxT"], 1)

            def transpose_stats(tile):
                done(pe, "varred2", tile)
                for c in range(4):
                    last = pe.transpose(bank[0][:, c * P:(c + 1) * P], mean_var[:, c // 2, (c % 2) * P:(c % 2 + 1) * P], ident)
                last.then_inc(S["statT"], 1)

            def project_stats(tile):
                p = tile[1]
                done(pe, "statevac", tile)
                done(pe, "maxq", tile)
                done(pe, "stated1", tile, 1)
                for c in range(6):
                    last = pe.matmul(bank[4][:, 0:D], stats[p][:, c, :], sproj[:, c, :], start=(c == 0), stop=(c == 5))
                last.then_inc(S["sprojed"], 1)

            def transpose_a(tile):
                done(pe, "a_ined", tile)
                for c in range(2):
                    last = pe.transpose(bank[4][:, c * P:(c + 1) * P], a_in[:, c * P:(c + 1) * P], ident)
                last.then_inc(S["aTed"], 1)

            def linear(to, w):
                for c in range(2):
                    last = pe.matmul(to, aT[:, c, :], w[:, c, :], start=(c == 0), stop=(c == 1))
                return last

            def query_key(tile):
                done(pe, "aTevac", tile)
                linear(bank[4][:, :], wq).then_inc(S["qed"], 1)
                done(pe, "qsed", tile, 1)
                linear(bank[5][:, :], wk).then_inc(S["ked"], 1)

            def value(tile):
                done(pe, "qbed", tile)
                linear(bank[4][:, :], wv).then_inc(S["ved"], 1)

            def transpose_q(tile):
                done(pe, "kbed", tile)
                for c in range(NC):
                    last = pe.transpose(bank[5][:, c * P:(c + 1) * P], qb[:, c * P:(c + 1) * P], ident)
                last.then_inc(S["qTed"], 1)

            def transpose_u(tile):
                done(pe, "ued", tile)
                for c in range(NC):
                    last = pe.transpose(bank[4][:, c * P:(c + 1) * P], u[:, c * P:(c + 1) * P], ident)
                last.then_inc(S["uTed"], 1)

            def project_out(tile):
                p = tile[1]
                done(pe, "oTed", tile)
                done(pe, "gTevac", tile, 1)
                for c in range(NC):
                    last = pe.matmul(bank[6][:, 0:D], oT[p][:, c, :], wo[:, c, :], start=(c == 0), stop=(c == NC - 1))
                last.then_inc(S["woed"], 1)

            def transpose_z(tile):
                done(pe, "zed", tile)
                done(pe, "h3ed", tile, 1)
                for c in range(2):
                    last = pe.transpose(bank[7][:, c * P:(c + 1) * P], z[:, c * P:(c + 1) * P], ident)
                last.then_inc(S["zTed"], 1)

            def ffn_up(tile):
                done(pe, "zTevac", tile)
                for c in range(2):
                    last = pe.matmul(bank[6][:, 0:E + D], zT[:, c, :], gate_up1[:, c, :], start=(c == 0), stop=(c == 1))
                last.then_inc(S["ffned1"], 1)
                done(pe, "zfirst", tile)
                for c in range(2):
                    last = pe.matmul(bank[7][:, 0:D], zT[:, c, :], up3[:, c, :], start=(c == 0), stop=(c == 1))
                last.then_inc(S["ffned3"], 1)

            def transpose_g(tile):
                done(pe, "g2ed", tile)
                for c in range(2):
                    last = pe.transpose(bank[6][:, c * P:(c + 1) * P], g2[:, c * P:(c + 1) * P], ident)
                last.then_inc(S["gTed"], 1)

            def ffn_down(tile):
                done(pe, "gTevac", tile)
                for c in range(2):
                    last = pe.matmul(bank[7][:, 0:D], gT[:, c, :], down[:, c, :], start=(c == 0), stop=(c == 1))
                last.then_inc(S["downed"], 1)

            def period(A, B, C):
                if C:
                    project_out(C)
                if B:
                    project_stats(B)
                if A:
                    logit_max_rows(A)
                    block_max_cols(A)
                if C:
                    transpose_z(C)
                    ffn_up(C)
                if B:
                    transpose_a(B)
                    query_key(B)
                if A:
                    transpose_maxima(A)
                    block_sums(A)
                if B:
                    value(B)
                if C:
                    transpose_g(C)
                    ffn_down(C)
                if B:
                    transpose_q(B)
                if A:
                    weighted_sums(A)
                if B:
                    transpose_u(B)
                if A:
                    transpose_stats(A)

            def table():
                done(pe, "zfirst", tile_of(0, E // 2 - 1))
                for b in range(4):
                    w = (w1, w3)[b // 2]
                    for c in range(2):
                        last = pe.matmul(bank[b][0:E, :], z_first[:, c, 0:E], w[:, c, (b % 2) * 4:(b % 2 + 1) * 4, :],
                                         start=(c == 0), stop=(c == 1))
                last.then_inc(S["tabbed"], 1)

            def routed(tile, first):
                t, p, n = tile
                done(pe, "pairwed", tile)
                done(pe, "pairTevac", tile, 2)
                pe.transpose(bank[1 + p][:, 0:P], pairs_w[p][:].rearrange("p s e g -> p (s e g)"), ident).then_inc(S["pairTed"], 1)
                done(pe, "pairTevac", tile)
                done(pe, "r2ed", tile, 2)
                for s in range(2):
                    last = pe.matmul(bank[4 + 2 * p + s][:, 0:2 * HID], pairs_wT[p][s * PAIRS:(s + 1) * PAIRS, :],
                                     tab[s * PAIRS:(s + 1) * PAIRS, :, :].rearrange("p k n -> p (k n)"), start=True, stop=True)
                last.then_inc(S["looked"], 1)
                done(pe, "r2ed", tile)
                done(pe, "paired", tile)
                for s in range(2):
                    last = pe.matmul(bank[0][s * PAIRS:(s + 1) * PAIRS, 0:HID], pairs[p][:, s].rearrange("p e g -> p (e g)"),
                                     r2[p][:, s, :], start=first, stop=True, skip_group_check=True)
                last.then_inc(S["acced"], 1)

            pe.wait_ge(weights_in, ALL_WEIGHTS)
            pe.wait_ge(setup_dve, 1)
            periods(pe, period, table)
            pe.wait_ge(route, COUNT_READY)
            pe.matmul(bank[3][:, 0:E], ones, mine[:], start=True, stop=True).then_inc(counted, 1)
            pe.wait_ge(tab_in, 64)
            done(pe, "tabrowed", tile_of(0, 0))
            routed_tiles(pe, routed)
            pe.wait_ge(hsummed, 1)
            pe.transpose(bank[1][:, 0:P], hsum[:], ident).then_inc(hsumT_pe, 1)
            pe.wait_ge(rouT, 1)
            for g in range(E):
                last = pe.matmul(bank[3][0:E, 0:D], hsumT[:, g:PAIRS:E], w2[:, g, :], start=(g == 0), stop=(g == E - 1))
            last.then_inc(final_pe, 1)

        @block.vector
        def _(dve):
            def dots(tile, part):
                t, p, n = tile
                if part == 0:
                    dve.wait_ge(x_in[p], 64 * (n + 1))
                done(dve, f"dot{(part - 1) % 4}", tile, 1 if part == 0 else 0)
                for c in range(part * JR, (part + 1) * JR):
                    last = dve.tensor_tensor_reduce(out=product[:, c % JR, :], in0=xx[p][:, 0, c * D:(c + 1) * D], in1=wproj[:],
                                                    scale=1.0, scalar=wproj_b[:, 0:1], op0=ALU.mult, op1=ALU.add,
                                                    accum_out=logit[:, c:c + 1])
                last.then_inc(S[f"dot{part}"], 1)

            def maxima(tile):
                p = tile[1]
                dve.wait_ge(x_in[p], 64 * (tile[2] + 1))
                rows = xx[p][:, 0, :].rearrange("p (s n) -> p s n", s=ST)
                dve.tensor_tensor(max2[:], rows[:, :, 0:2 * D], rows[:, :, 2 * D:4 * D], ALU.max).then_inc(S["maxed2"], 1)
                done(dve, "maxed2", tile)
                done(dve, "maxT", tile, 1)
                dve.tensor_tensor(max1[:], max2[:, :, 0:D], max2[:, :, D:2 * D], ALU.max).then_inc(S["maxed1"], 1)

            def maxima_of_blocks(tile):
                done(dve, "maxT", tile)
                done(dve, "sprojed", tile, 2)
                dve.tensor_reduce(stats[tile[1]][:, 4:6, :], psum[:, 2:4, :].rearrange("p c (n q) -> p c n q", q=Q),
                                  AX.X, ALU.max).then_inc(S["maxq"], 1)

            def logit_max_of_rows(tile):
                done(dve, "dot3", tile)
                dve.tensor_reduce(logit_max[:], logit[:].rearrange("p (s j) -> p s j", j=JR), AX.X, ALU.max).then_inc(S["lmaxed"], 1)

            def logit_max_of_blocks(tile):
                done(dve, "lmaxT", tile)
                dve.tensor_reduce(block_max[:], bank[1][0:ST, 0:P].rearrange("s (b q) -> s b q", q=Q), AX.X, ALU.max).then_inc(S["bmaxed0"], 1)
                done(dve, "bmaxed0", tile)
                dve.tensor_copy(block_max4[:], block_max[:].rearrange("s (b a) -> s b a", a=1).broadcast_to([ST, BL, Q])).then_inc(S["bmaxed"], 1)

            def per_block(ap):
                return ap.rearrange("p (s a) -> p s a", a=1).broadcast_to([P, ST, JR])

            def shift_logits(tile):
                done(dve, "bmaxT", tile)
                dve.tensor_tensor(shifted[:].rearrange("p (s j) -> p s j", j=JR), logit[:].rearrange("p (s j) -> p s j", j=JR),
                                  per_block(bank[1][:, P:P + ST]), ALU.subtract).then_inc(S["shifted"], 1)

            def sum_expo(tile):
                done(dve, "exped", tile)
                dve.tensor_reduce(expo_sum[:], expo[:].rearrange("p (s j) -> p s j", j=JR), AX.X, ALU.add).then_inc(S["esummed"], 1)

            def normalise(tile):
                done(dve, "denned", tile)
                dve.reciprocal(inv_sum[:], bank[1][:, P:P + ST]).then_inc(S["rdenned"], 1)
                done(dve, "rdenned", tile)
                dve.tensor_tensor(weight[:].rearrange("p (s j) -> p s j", j=JR), expo[:].rearrange("p (s j) -> p s j", j=JR),
                                  per_block(inv_sum[:]), ALU.mult).then_inc(S["weighted"], 1)

            def variance(tile):
                done(dve, "msqed", tile)
                dve.tensor_tensor(mean_var[:, 1, :], bank[0][:, D:2 * D], mean_sq[:], ALU.subtract).then_inc(S["varred"], 1)
                done(dve, "varred", tile)
                dve.tensor_scalar(mean_var[:, 1, :], mean_var[:, 1, :], 0.0, VAR_EPS, ALU.max, ALU.add).then_inc(S["varred2"], 1)

            def norm_stats(i, src, tile, ready):
                done(dve, ready, tile)
                dve.bn_stats(bn[i][:], src).then_inc(S[f"bn{i}"], 1)
                done(dve, f"bn{i}", tile)

            def norm_mean(i, tile):
                dve.bn_aggr(mv[i][:], bn[i][:]).then_inc(S[f"mv{i}"], 1)

            def token(tile):
                done(dve, "sprojed", tile)
                dve.tensor_tensor(h0[:], bank[4][:, 0:D], sproj_b[:], ALU.add).then_inc(S["h0ed"], 1)
                norm_stats(0, h0[:], tile, "h0ed")

            def token_scale(tile):
                done(dve, "mv0", tile)
                dve.scalar_tensor_tensor(out=h0c[:], in0=h0[:], scalar=mv[0][:, 0:1], in1=ln_g[:], op0=ALU.subtract, op1=ALU.mult).then_inc(S["h0ced"], 1)

            def token_out(tile):
                p = tile[1]
                done(dve, "rstd0", tile)
                done(dve, "posb", tile)
                done(dve, "h0ced", tile)
                done(dve, "h1bed", tile, 2)
                dve.scalar_tensor_tensor(out=h1[p][:], in0=h0c[:], scalar=rstd[0][:, 0:1], in1=pos_b[:], op0=ALU.mult, op1=ALU.add).then_inc(S["h1ed"], 1)
                norm_stats(1, h1[p][:], tile, "h1ed")

            def attention_in(tile):
                done(dve, "rstd1", tile)
                dve.tensor_scalar(a_in[:], h1[tile[1]][:], mv[1][:, 0:1], rstd[1][:, 0:1], ALU.subtract, ALU.mult).then_inc(S["a_ined"], 1)

            def query_key_bias(tile):
                done(dve, "qed", tile)
                done(dve, "qTed", tile, 1)
                done(dve, "kqed", tile, 1)
                dve.tensor_tensor(qb[:], bank[4][:, :], bq[:], ALU.add).then_inc(S["qbed"], 1)
                done(dve, "ked", tile)
                dve.tensor_tensor(kb[:], bank[5][:, :], bk[:], ALU.add).then_inc(S["kbed"], 1)

            def scores(tile):
                done(dve, "kqed", tile)
                dve.tensor_reduce(score[:], kq[:].rearrange("p (h d) -> p h d", h=HEADS), AX.X, ALU.add).then_inc(S["scored"], 1)
                done(dve, "scored", tile)
                dve.tensor_reduce(neg_max[:], score[:], AX.X, ALU.max, negate=True).then_inc(S["nmaxed"], 1)

            def head_softmax(tile):
                done(dve, "eed", tile)
                dve.reciprocal(s_inv[:], s_sum[:]).then_inc(S["sinved"], 1)
                done(dve, "sinved", tile)
                dve.tensor_scalar(attn[:], e_score[:], s_inv[:, 0:1], None, ALU.mult).then_inc(S["attned"], 1)

            def advance_state(tile):
                p = tile[1]
                done(dve, "uTed", tile)
                done(dve, "stated1", tile, 1)
                for c in range(NC):
                    last = dve.scalar_tensor_tensor(out=state[p][:, c, 0:CLIPS], in0=state[1 - p][:, c, CLIPS:P], scalar=decay_cols[:, c:c + 1],
                                                    in1=bank[4][:, c * P:c * P + CLIPS], op0=ALU.mult, op1=ALU.add)
                last.then_inc(S["stated0"], 1)
                done(dve, "stated0", tile)
                for c in range(NC):
                    last = dve.scalar_tensor_tensor(out=state[p][:, c, CLIPS:P], in0=state[p][:, c, 0:CLIPS], scalar=decay_cols[:, c:c + 1],
                                                    in1=bank[4][:, c * P + CLIPS:(c + 1) * P], op0=ALU.mult, op1=ALU.add)
                last.then_inc(S["stated1"], 1)

            def query_state(tile):
                done(dve, "stated1", tile)
                done(dve, "tanhed", tile)
                done(dve, "oTed", tile, 1)
                dve.tensor_tensor(qs[:], bank[5][:, :].rearrange("p (c n) -> p c n", c=NC), state[tile[1]][:], ALU.mult).then_inc(S["qsed"], 1)

            def attention_out(tile):
                done(dve, "woed", tile)
                dve.tensor_tensor(o_raw[:], bank[6][:, 0:D], bo[:], ALU.add).then_inc(S["oed"], 1)
                norm_stats(2, o_raw[:], tile, "oed")

            def attention_scale(tile):
                done(dve, "mv2", tile)
                dve.scalar_tensor_tensor(out=o_c[:], in0=o_raw[:], scalar=mv[2][:, 0:1], in1=att_g[:], op0=ALU.subtract, op1=ALU.mult).then_inc(S["oced"], 1)

            def residual(tile):
                done(dve, "rstd2", tile)
                done(dve, "h1bed", tile)
                done(dve, "oced", tile)
                dve.scalar_tensor_tensor(out=h2[:], in0=o_c[:], scalar=rstd[2][:, 0:1], in1=h1b[:], op0=ALU.mult, op1=ALU.add).then_inc(S["h2ed"], 1)
                norm_stats(3, h2[:], tile, "h2ed")

            def ffn_in(tile):
                done(dve, "rstd3", tile)
                dve.tensor_scalar(z[:], h2[:], mv[3][:, 0:1], rstd[3][:, 0:1], ALU.subtract, ALU.mult).then_inc(S["zed"], 1)

            def silu_product(tile):
                done(dve, "htanh", tile)
                dve.scalar_tensor_tensor(out=g1[:], in0=half_tanh[:], scalar=1.0, in1=bank[6][:, E:E + D], op0=ALU.add, op1=ALU.mult).then_inc(S["g1ed"], 1)
                done(dve, "ffned3", tile)
                done(dve, "g1ed", tile)
                dve.scalar_tensor_tensor(out=g2[:], in0=g1[:], scalar=0.5, in1=bank[7][:, 0:D], op0=ALU.mult, op1=ALU.mult).then_inc(S["g2ed"], 1)

            def result(tile):
                t, p, n = tile
                done(dve, "downed", tile)
                if not (isinstance(n, int) and n < 1):
                    dve.wait_ge(stored[p], 32 * n)
                dve.tensor_tensor(h3[p][:], bank[7][:, 0:D], h2[:], ALU.add).then_inc(S["h3ed"], 1)

            def period(A, B, C):
                if C:
                    attention_out(C)
                if A:
                    dots(A, 0)
                if C:
                    norm_mean(2, C)
                    attention_scale(C)
                if B:
                    token(B)
                if A:
                    dots(A, 1)
                if B:
                    norm_mean(0, B)
                    token_scale(B)
                if C:
                    residual(C)
                if A:
                    dots(A, 2)
                if C:
                    norm_mean(3, C)
                if B:
                    token_out(B)
                if A:
                    dots(A, 3)
                if B:
                    norm_mean(1, B)
                if A:
                    logit_max_of_rows(A)
                    logit_max_of_blocks(A)
                    shift_logits(A)
                if C:
                    ffn_in(C)
                if B:
                    attention_in(B)
                if A:
                    maxima(A)
                    sum_expo(A)
                    normalise(A)
                if B:
                    query_key_bias(B)
                if C:
                    silu_product(C)
                if A:
                    maxima_of_blocks(A)
                if B:
                    scores(B)
                    head_softmax(B)
                if C:
                    result(C)
                if B:
                    advance_state(B)
                    query_state(B)
                if A:
                    variance(A)

            def routed(tile, first):
                t, p, n = tile
                done(dve, "pairTed", tile, 2)
                dve.tensor_tensor(pairs_w[p][:],
                                  chosen_w[:, bass.ds(2 * t, 2), :].rearrange("p s (e a) -> p s e a", a=1).broadcast_to([P, 2, E, E]),
                                  segment[:, bass.ds(2 * t, 2), :].rearrange("p s (a g) -> p s a g", a=1).broadcast_to([P, 2, E, E]),
                                  ALU.mult).then_inc(S["pairwed"], 1)
                done(dve, "rtanhed", tile)
                ab = psum[:, 4 + 2 * p:6 + 2 * p, 0:2 * HID].rearrange("p s (k n) -> p k s n", k=2)
                dve.scalar_tensor_tensor(out=r1[p][:], in0=r_tanh[p][:], scalar=1.0, in1=ab[:, 0], op0=ALU.add, op1=ALU.mult).then_inc(S["r1ed"], 1)
                done(dve, "r1ed", tile)
                done(dve, "acced", tile, 2)
                dve.scalar_tensor_tensor(out=r2[p][:], in0=r1[p][:], scalar=0.5, in1=ab[:, 1], op0=ALU.mult, op1=ALU.mult).then_inc(S["r2ed"], 1)

            dve.memset(state[1][:], 0.0)
            dve.wait_ge(weights_in, ALL_WEIGHTS)
            dve.wait_ge(setup_act, 2)
            dve.tensor_scalar(decay_cols[:], alpha_cols[:], 0.5, 0.5, ALU.mult, ALU.add)
            dve.tensor_scalar(aug_cols[:], aug_cols[:], 0.5, None, ALU.mult)
            dve.tensor_scalar(wk[:], wk[:], HD ** -0.5, None, ALU.mult)
            dve.tensor_scalar(bk[:], bk[:], HD ** -0.5, None, ALU.mult)
            dve.tensor_scalar(keep_row[:], keep_row[:], -0.5, 0.5, ALU.mult, ALU.add).then_inc(route, 1)
            dve.wait_ge(route, 1)
            dve.tensor_tensor(bv[:], bv[:], keep_row[:], ALU.mult)
            for c in range(2):
                last = dve.tensor_tensor(wv[:, c, :], wv[:, c, :], keep_row[:], ALU.mult)
            last.then_inc(setup_dve, 1)
            dve.wait_ge(setup_dve, 1)
            periods(dve, period)

            steps = [1]

            def link(instruction):
                steps[0] += 1
                instruction.then_inc(route, 1)
                dve.wait_ge(route, steps[0])

            def cols(ap, n):
                return ap.rearrange("p (t a) -> p t a", a=1).broadcast_to([P, TILES, n])

            def ranks(out_rank, values, n, before):
                gt = cmp_gt[:, 0:TILES * n * n].rearrange("p (t a b) -> p t a b", a=n, b=n)
                ge = cmp_ge[:, 0:TILES * n * n].rearrange("p (t a b) -> p t a b", a=n, b=n)
                other = values.rearrange("p t (a b) -> p t a b", a=1).broadcast_to([P, TILES, n, n])
                own = values.rearrange("p t (a b) -> p t a b", b=1).broadcast_to([P, TILES, n, n])
                dve.tensor_tensor(gt, other, own, ALU.is_gt)
                link(dve.tensor_tensor(ge, other, own, ALU.is_ge))
                link(dve.tensor_tensor(ge, ge, before.rearrange("p (z a b) -> p z a b", z=1, a=n).broadcast_to([P, TILES, n, n]), ALU.mult))
                link(dve.tensor_tensor(gt, gt, ge, ALU.max))
                link(dve.tensor_reduce(out_rank, gt, AX.X, ALU.add))

            done(dve, "gated", tile_of(0, TILES - 1))
            link(dve.tensor_reduce(t1[:], gate[:], AX.X, ALU.max))
            link(dve.tensor_tensor(sc[:], gate[:], cols(t1[:], E), ALU.subtract))
            assert steps[0] == GATE_SHIFTED
            dve.wait_ge(gate_exp, 1)
            link(dve.tensor_reduce(t1[:], sc[:], AX.X, ALU.add))
            link(dve.reciprocal(t1[:], t1[:]))
            link(dve.tensor_tensor(sc[:], sc[:], cols(t1[:], E), ALU.mult))
            link(dve.tensor_tensor(s2[:], sc[:], ebias[:].rearrange("p (a e) -> p a e", a=1).broadcast_to([P, TILES, E]), ALU.add))
            link(dve.tensor_reduce(gsum[:], s2[:].rearrange("p t (g m) -> p t g m", m=E // G), AX.X, ALU.add))
            ranks(grank[:], gsum[:], G, const[:, C_LT4:C_LT4 + 16])
            link(dve.tensor_scalar(grank[:], grank[:], 2.0, -1e30, ALU.is_ge, ALU.mult))
            link(dve.tensor_tensor(s3[:].rearrange("p t (g m) -> p t g m", m=E // G), s2[:].rearrange("p t (g m) -> p t g m", m=E // G),
                                   grank[:].rearrange("p t (g a) -> p t g a", a=1).broadcast_to([P, TILES, G, E // G]), ALU.add))
            ranks(rank[:], s3[:], E, const[:, C_LT8:C_LT8 + 64])
            by_slot = chosen[:].rearrange("p (t s) e -> p t s e", s=2)
            for s in range(2):
                last = dve.tensor_scalar(by_slot[:, :, s, :], rank[:], float(s), None, ALU.is_equal)
            link(last)
            link(dve.memset(chosen[CLIPS:P, 2 * TILES - 2:2 * TILES, :], 0.0))
            link(dve.tensor_reduce(mine[:], chosen[:].rearrange("p n e -> p e n"), AX.X, ALU.add))
            assert steps[0] == COUNT_READY
            for s in range(2):
                last = dve.tensor_tensor(chosen_w[:].rearrange("p (t s) e -> p t s e", s=2)[:, :, s, :], by_slot[:, :, s, :], sc[:], ALU.mult)
            link(last)
            dve.wait_ge(counted, 1)
            link(dve.tensor_copy(count[:], bank[3][:, 0:E]))
            link(dve.tensor_tensor_scan(seg_end[:], ones[:, 0:E], count[:], 0.0, ALU.mult, ALU.add))
            link(dve.tensor_tensor(seg_start[:], seg_end[:], count[:], ALU.subtract))
            position = const[:, C_POS:C_POS + 2 * TILES].rearrange("p (n a) -> p n a", a=1).broadcast_to([P, 2 * TILES, E])
            bounds = lambda ap: ap.rearrange("p (a e) -> p a e", a=1).broadcast_to([P, 2 * TILES, E])
            dve.tensor_tensor(segment[:], position, bounds(seg_start[:]), ALU.is_ge)
            link(dve.tensor_tensor(seg_hi[:], position, bounds(seg_end[:]), ALU.is_lt))
            link(dve.tensor_tensor(segment[:], segment[:], seg_hi[:], ALU.mult))
            assert steps[0] == ROUTE_DONE
            routed_tiles(dve, routed)
            dve.wait_ge(hsumT_act, 1)
            dve.tensor_tensor(hsumT[:], bank[1][:, PAIRS:2 * PAIRS], hsumT0[:], ALU.add).then_inc(rouT, 1)
            dve.wait_ge(final_pe, 1)
            dve.wait_ge(first8_in, 16)
            dve.tensor_tensor(first8_out[:], bank[3][0:E, 0:D], first8[:], ALU.add).then_inc(final_dve, 1)


GATE_SHIFTED, COUNT_READY, ROUTE_DONE = 3, 21, 27

SHAPE = (CLIPS, NBLK, D)


def kernel(**inputs):
    import concourse.bacc as bacc
    from concourse.bass_utils import run_bass_kernel_spmd

    arrays = {n: np.ascontiguousarray(v) for n, v in inputs.items()}
    arrays["w_gate_T"] = np.ascontiguousarray(arrays.pop("L0_ffn_w_gate").T)
    for n in ("sw1", "sw2", "sw3"):
        arrays[n + "_T"] = np.ascontiguousarray(arrays.pop("L0_ffn_" + n).T)
    arrays["alpha_cols"] = np.ascontiguousarray(arrays["L0_attn_alpha"].reshape(NC, P).T)
    arrays["aug_cols"] = np.ascontiguousarray(arrays.pop("L0_attn_aug_param").reshape(NC, P).T)
    arrays["const"] = constants()
    arrays["zeros"] = np.zeros((P, JR * D), np.float32)
    nc = bacc.Bacc("TRN2", target_bir_lowering=False, num_devices=1)
    aps = {n: nc.dram_tensor("in_" + n, v.shape, mybir.dt.from_np(v.dtype), kind="ExternalInput").ap() for n, v in arrays.items()}
    out = nc.dram_tensor("tower_out", SHAPE, F32, kind="ExternalOutput").ap()
    audio_tower(nc, aps, out)
    r = run_bass_kernel_spmd(nc, [{"in_" + n: v for n, v in arrays.items()}], core_ids=[0])
    return r.results[0]["tower_out"]
```

```python
from contextlib import ExitStack

import numpy as np

import concourse.bass as bass
from concourse import mybir

F32 = mybir.dt.float32
ALU = mybir.AluOpType
ACT = mybir.ActivationFunctionType
AX = mybir.AxisListType

P = 128
CLIPS, ROWS, D = 64, 750, 256
BLOCK = 16
NBLK = -(-ROWS // BLOCK)
TILES = -(-NBLK // 2)
ST = 4
JR = 4
Q = BLOCK // JR
BL = P // Q
HEADS, HD = 8, 64
CH = HEADS * HD
NC = CH // P
E, HID = 8, 128
G = 4
PAIRS = E * E
POS_ROWS = NBLK + 1
LN_TOK, LN_ATT, LN_H, VAR_EPS = 1e-5, 1e-6, 1e-5, 1e-8

C_ID, C_ONES, C_BLK, C_MASK, C_HALF = 0, 128, 256, 384, 416
C_EPS = C_HALF + 1
C_VAR, C_NEG = C_EPS + 4, C_EPS + 5
C_POS = C_NEG + 1
C_LT8 = C_POS + 2 * TILES
C_LT4 = C_LT8 + 64
C_END = C_LT4 + 16


MATS = [(6, D), (2, CH), (2, CH), (2, CH), (NC, D), (2, E + D), (2, D), (2, D), (NC,), (NC,)]
ROWVECS = [D] * 6 + [CH] * 4 + [E]


def constants():
    p = np.arange(P)
    c = np.zeros((P, C_END), np.float32)
    c[:, C_ID:C_ID + P] = np.eye(P)
    c[:, C_ONES:C_ONES + P] = 1.0
    c[:, C_BLK:C_BLK + P] = p[:, None] // Q == p[None, :] // Q
    c[:, C_MASK:C_MASK + BL] = p[:, None] // Q == np.arange(BL)[None, :]
    c[:, C_HALF] = -0.5
    c[:, C_EPS:C_EPS + 4] = (LN_TOK, LN_H, LN_ATT, LN_H)
    c[:, C_VAR], c[:, C_NEG] = VAR_EPS, -1.0
    t = np.arange(TILES)[None, :, None]
    s = np.arange(2)[None, None, :]
    token = (p[:, None, None] % CLIPS) * NBLK + 2 * t + p[:, None, None] // CLIPS
    c[:, C_POS:C_POS + 2 * TILES] = (2 * token + s).reshape(P, -1)
    c[:, C_LT8:C_LT8 + 64] = (np.arange(8)[None, :] < np.arange(8)[:, None]).reshape(-1)
    c[:, C_LT4:C_LT4 + 16] = (np.arange(4)[None, :] < np.arange(4)[:, None]).reshape(-1)
    return c


def audio_tower(nc, a, out):
    x = a["x"]
    with ExitStack() as ctx:
        def sb(name, *shape):
            return ctx.enter_context(nc.sbuf_tensor(name, list(shape), F32))

        def sem(name):
            return ctx.enter_context(nc.semaphore(name))

        const = sb("const", P, C_END)
        ident = const[:, C_ID:C_ID + P]
        ones = const[:, C_ONES:C_ONES + P]
        same_block = const[:, C_BLK:C_BLK + P]
        block_mask = const[:, C_MASK:C_MASK + BL]
        minus_half = const[:, C_HALF:C_HALF + 1]
        wproj, wproj_b = sb("wproj", P, D), sb("wproj_b", P, 1)
        zeros = a["zeros"]

        def views(tensor, parts):
            at, out = 0, []
            for shape in parts:
                n = int(np.prod(shape))
                part = tensor[:, at:at + n]
                if len(shape) > 1:
                    dims = " ".join("abc"[:len(shape)])
                    part = part.rearrange(f"p ({dims}) -> p {dims}", **dict(zip("abc", shape)))
                out.append(part)
                at += n
            return out

        mats = sb("mats", P, sum(int(np.prod(m)) for m in MATS))
        sproj, wq, wk, wv, wo, gate_up1, up3, down, alpha_cols, aug_cols = views(mats, MATS)
        rows = sb("rows", P, sum(ROWVECS))
        sproj_b, ln_g, ln_b, bo, att_g, att_b, bq, bk, bv, keep_row, ebias = views(rows, [(n,) for n in ROWVECS])
        experts = sb("experts", P, 2 * E * D)
        w1, w3 = views(experts, [(2, E, HID), (2, E, HID)])
        decay_cols = sb("decay_cols", P, NC)
        decay = sb("decay", P, NC, CLIPS)

        xx = [sb(f"xx{i}", P, 2, ST * JR * D) for i in range(2)]
        product = sb("product", P, JR, D)
        products_of = {part: sb(f"products{part}", P, JR, D) for part in (2, 3)}
        max2, max1 = sb("max2", P, ST, 2 * D), sb("max1", P, ST, D)
        logit = sb("logit", P, ST * JR)
        logit_max, block_max, block_max4 = sb("logit_max", P, ST), sb("block_max", ST, BL), sb("block_max4", ST, BL, Q)
        shifted, expo, weight = sb("shifted", P, ST * JR), sb("expo", P, ST * JR), sb("weight", P, ST * JR)
        expo_sum, inv_sum = sb("expo_sum", P, ST), sb("inv_sum", P, ST)
        spread = sb("spread", P, ST, JR, BL)
        mean_var, mean_sq = sb("mean_var", P, 2, D), sb("mean_sq", P, D)
        stats = [sb(f"stats{i}", P, 6, P) for i in range(2)]
        pos = [sb(f"pos{i}", P, D) for i in range(2)]
        pos_b = sb("pos_b", P, D)
        h0 = sb("h0", P, D)
        bn = [sb(f"bn{i}", P, 6) for i in range(4)]
        mv = [sb(f"mv{i}", P, 2) for i in range(4)]
        neg_mean = [sb(f"neg_mean{i}", P, 1) for i in range(4)]
        offset = [sb(f"offset{i}", P, 1) for i in range(4)]
        ve = [sb(f"ve{i}", P, 1) for i in range(4)]
        rstd = [sb(f"rstd{i}", P, 1) for i in range(4)]
        h1 = [sb(f"h1_{i}", P, D) for i in range(2)]
        a_in, aT = sb("a_in", P, D), sb("aT", P, 2, P)
        qb, kb, vb = sb("qb", P, CH), sb("kb", P, CH), sb("vb", P, CH)
        score, neg_max, e_score = sb("score", P, HEADS), sb("neg_max", P, 1), sb("e_score", P, HEADS)
        s_sum, s_inv, attn = sb("s_sum", P, 1), sb("s_inv", P, 1), sb("attn", P, HEADS)
        u = sb("u", P, CH)
        carried = sb("carried", P, NC, CLIPS)
        decayed = sb("decayed", P, NC, CLIPS)
        aug = sb("aug", P, NC, P)
        state = [sb(f"state{i}", P, NC, P) for i in range(2)]
        qs = sb("qs", P, NC, P)
        oT = [sb(f"oT{i}", P, NC, P) for i in range(2)]
        h1b, o_raw, h2 = sb("h1b", P, D), sb("o_raw", P, D), sb("h2", P, D)
        z, zT = sb("z", P, D), sb("zT", P, 2, P)
        z_first = sb("z_first", P, 2, 2 * TILES)
        gate = sb("gate", P, TILES, E)
        half_tanh, g2, gT = sb("half_tanh", P, D), sb("g2", P, D), sb("gT", P, 2, P)
        h3 = [sb(f"h3_{i}", P, D) for i in range(2)]

        spares = [b[:].rearrange("p k n -> p (k n)") for b in xx]
        used = [0]

        def carve(name, *shape):
            size = int(np.prod(shape[1:]))
            if used[0] + size > 2 * ST * JR * D:
                spares.pop(0)
                used[0] = 0
            part = spares[0][0:shape[0], used[0]:used[0] + size]
            used[0] += size
            if len(shape) == 2:
                return part
            dims = " ".join("abc"[:len(shape) - 1])
            return part.rearrange(f"p ({dims}) -> p {dims}", **dict(zip("abc", shape[1:])))

        w2 = carve("w2", P, E, D)
        sc, s2, s3 = carve("sc", P, TILES, E), carve("s2", P, TILES, E), carve("s3", P, TILES, E)
        t1, gsum, grank = carve("t1", P, TILES), carve("gsum", P, TILES, G), carve("grank", P, TILES, G)
        cmp_gt, cmp_ge = carve("cmp_gt", P, TILES * E * E), carve("cmp_ge", P, TILES * E * E)
        rank = carve("rank", P, TILES, E)
        chosen, chosen_w, segment, seg_hi = (carve(n, P, 2 * TILES, E) for n in ("chosen", "chosen_w", "segment", "seg_hi"))
        slot_w = carve("slot_w", P, 2 * TILES)
        mine, count, seg_end, seg_start = (carve(n, P, E) for n in ("mine", "count", "seg_end", "seg_start"))
        tab_rows = carve("tab_rows", E, 2, E * HID)
        tab = carve("tab", P, 2, HID)
        pairs, pairs_w = ([carve(f"{n}{i}", P, 2, E, E) for i in range(2)] for n in ("pairs", "pairs_w"))
        pairs_wT = [carve(f"pairs_wT{i}", P, P) for i in range(2)]
        r_tanh, r1, r2 = ([carve(f"{n}{i}", P, 2, HID) for i in range(2)] for n in ("r_tanh", "r1_", "r2_"))
        hsum, hsumT0, hsumT = carve("hsum", P, HID), carve("hsumT0", P, PAIRS), carve("hsumT", P, PAIRS)
        first8, first8_out = carve("first8", E, D), carve("first8_out", E, D)

        psum = ctx.enter_context(nc.psum_tensor("psum", [P, 8, 512], F32))
        bank = [psum[:, i, :] for i in range(8)]

        early_in, mats_in, experts_in = sem("early_in"), sem("mats_in"), sem("experts_in")
        setup_act, setup_dve, setup_pool = sem("setup_act"), sem("setup_dve"), sem("setup_pool")
        x_in = [sem(f"x_in{i}") for i in range(2)]
        pos_in = [sem(f"pos_in{i}") for i in range(2)]
        stored = [sem(f"stored{i}") for i in range(2)]
        names = """prod2 prod2b prod3 prod3b dot0 dot1 dot2 dot3 maxed2 maxed1 squared lmaxed lmaxT bmaxed0 bmaxed bmaxT shifted exped esummed denned rdenned
            weighted spreaded summed maxT maxq meaned msqed varred reluedv statT statevac
            sprojed bn0 mv0 nm0 ve0 rstd0 posb h0ced h1ed bn1 mv1 nm1 ve1 rstd1 off1 a_ined aTed aTevac qed ked ved
            qbed kbed vcopied vbed kqed scored nmaxed eed sinved attned ued qTed uTed tanhed auged
            carriedd stated0 decayedd stated1 qsed oTed
            woed h1bed bn2 mv2 ve2 rstd2 oced h2ed bn3 mv3 nm3 ve3 rstd3 off3 zed zTed zTevac zfirst
            ffned3 ffned1 gated htanh g1ed g2ed gTed gTevac downed h3ed""".split()
        names += "tabbed tabrowed paired pairwed pairTed pairTevac looked rtanhed r1ed r2ed acced".split()
        route, gate_exp, counted, rouT, hsummed, hsumT_pe, hsumT_act, final_pe, final_dve = (
            sem(n) for n in "route gate_exp counted rouT hsummed hsumT_pe hsumT_act final_pe final_dve".split())
        last_in, tab_in, first8_in, first8_stored = (sem(n) for n in "last_in tab_in first8_in first8_stored".split())
        S = {n: sem("s_" + n) for n in names}

        def done(eng, name, tile, lag=0):
            value = tile[0] + 1 - lag
            if isinstance(value, int) and value < 1:
                return
            eng.wait_ge(S[name], value)

        block = ctx.enter_context(nc.Block())
        def tile_of(h, c):
            return (2 * h + c, c % 2, h + c // 2)

        def periods(eng, period, setup, drain=None, between=None):
            tiles = lambda k: [tile_of(0, k - d) if 0 <= k - d < TILES else None for d in range(3)]
            for k in range(4):
                period(*tiles(k))
                if k == 0:
                    setup()
            with eng.Fori(2, TILES // 2) as h:
                for c in range(2):
                    period(tile_of(h, c), tile_of(h, c - 1), tile_of(h, c - 2))
            if drain:
                drain(*tiles(TILES)[1:], tiles(TILES + 1)[2])
                return
            period(*tiles(TILES))
            if between:
                between()
            period(*tiles(TILES + 1))

        def routed_tiles(eng, routed):
            for t in range(2):
                routed(tile_of(0, t), t == 0)
            with eng.Fori(1, TILES // 2) as h:
                for c in range(2):
                    routed(tile_of(h, c), False)

        @block.sync
        def _(sp):
            def buffer_read(tile):
                for step in ("maxed2", "squared", "summed"):
                    done(sp, step, tile, 2)

            def load_x(tile):
                t, p, n = tile
                buffer_read(tile)
                for s in range(ST):
                    tl, bh = s // 2, s % 2
                    src = x[bh * BL:(bh + 1) * BL, bass.ds((2 * t + tl) * BLOCK, BLOCK), :]
                    sp.dma_start(xx[p][:, 0, s * JR * D:(s + 1) * JR * D],
                                 src.rearrange("b (q j) d -> b q (j d)", q=Q)).then_inc(x_in[p], 16)

            def load_last_x(tile):
                p = tile[1]
                start = (NBLK - 1) * BLOCK
                rows = ROWS - start - (Q - 1) * JR
                buffer_read(tile)
                for bh in range(2):
                    cols = xx[p][:, 0, bh * JR * D:(bh + 1) * JR * D]
                    for q in range(Q - 1):
                        sp.dma_start(cols[q:P:Q, :], x[bh * BL:(bh + 1) * BL, start + q * JR:start + (q + 1) * JR, :]
                                     .rearrange("b j d -> b (j d)")).then_inc(last_in, 16)
                    sp.dma_start(cols[Q - 1:P:Q, rows * D:], zeros[0:BL, rows * D:]).then_inc(last_in, 16)
                sp.wait_ge(last_in, 16 * 2 * Q)
                for bh in range(2):
                    sp.dma_start(xx[p][Q - 1:P:Q, 0, bh * JR * D:bh * JR * D + rows * D],
                                 x[bh * BL:(bh + 1) * BL, ROWS - rows:ROWS, :].rearrange("b j d -> b (j d)")).then_inc(x_in[p], 16)
                    sp.dma_start(xx[p][:, 0, (2 + bh) * JR * D:(3 + bh) * JR * D], zeros[:, :]).then_inc(x_in[p], 16)

            def load_pos(tile):
                t, p, n = tile
                done(sp, "posb", tile, 2)
                for tl in range(2):
                    sp.dma_start(pos[p][tl * CLIPS:(tl + 1) * CLIPS, :],
                                 a["L0_tok_pos_emb"][bass.ds(2 * t + tl, 1), :].broadcast_to([CLIPS, D])).then_inc(pos_in[p], 16)

            def store(tile, steps=2):
                t, p, n = tile
                done(sp, "h3ed", tile)
                for tl in range(steps):
                    sp.dma_start(out[:, bass.ds(2 * t + tl, 1), :].rearrange("b t d -> b (t d)"),
                                 h3[p][tl * CLIPS:(tl + 1) * CLIPS, :]).then_inc(stored[p], 16)

            sp.dma_start(const[:], a["const"]).then_inc(early_in, 16)
            sp.dma_start(wproj[:], a["L0_tok_w_proj_w"].rearrange("d a -> a d").broadcast_to([P, D])).then_inc(early_in, 16)
            sp.dma_start(wproj_b[:], a["L0_tok_w_proj_b"].rearrange("(a n) -> a n", a=1).broadcast_to([P, 1])).then_inc(early_in, 16)
            load_x(tile_of(0, 0))
            sp.dma_start(rows[:], a["rows"].broadcast_to([P, sum(ROWVECS)])).then_inc(mats_in, 16)
            sp.dma_start(mats[:], a["mats"]).then_inc(mats_in, 16)
            load_x(tile_of(0, 1))
            for k in range(4):
                load_x(tile_of(0, k + 2))
                load_pos(tile_of(0, k))
                if k >= 2:
                    store(tile_of(0, k - 2))
                if k == 2:
                    sp.dma_start(experts[:], a["experts"][:, 0:2 * E * D]).then_inc(experts_in, 16)
            with sp.Fori(2, TILES // 2 - 2) as h:
                for c in range(2):
                    load_x(tile_of(h, c + 2))
                    load_pos(tile_of(h, c))
                    store(tile_of(h, c - 2))
            for k in range(TILES - 4, TILES + 2):
                if k + 2 == TILES - 1:
                    load_last_x(tile_of(0, k + 2))
                elif k + 2 < TILES:
                    load_x(tile_of(0, k + 2))
                if k < TILES:
                    load_pos(tile_of(0, k))
                if k == TILES - 1:
                    for step in ("maxed2", "squared", "summed"):
                        done(sp, step, tile_of(0, k - 1))
                    sp.dma_start(w2.rearrange("p e d -> p (e d)"), a["experts"][:, 2 * E * D:]).then_inc(experts_in, 16)
                if k == TILES:
                    done(sp, "tabrowed", tile_of(0, 0))
                    for s in range(2):
                        for kind in range(2):
                            sp.dma_start(tab[s * PAIRS:(s + 1) * PAIRS, kind, :],
                                         tab_rows[:, kind, :].rearrange("e (g n) -> e g n", g=E)).then_inc(tab_in, 16)
                store(tile_of(0, k - 2), 1 if k - 2 == TILES - 1 else 2)
            sp.wait_ge(stored[0], 32 * (TILES // 2))
            sp.wait_ge(stored[1], 32 * (TILES // 2) - 16)
            sp.dma_start(first8[:], out[0, 0:E, :]).then_inc(first8_in, 16)
            sp.wait_ge(final_dve, 1)
            sp.dma_start(out[0, 0:E, :], first8_out[:]).then_inc(first8_stored, 16)
            sp.wait_ge(first8_stored, 16)

        @block.gpsimd
        def _(pool):
            def rstd_of(i, tile):
                done(pool, f"mv{i}", tile)
                if i in (1, 3):
                    pool.tensor_tensor(neg_mean[i][:], mv[i][:, 0:1], const[:, C_NEG:C_NEG + 1], ALU.mult).then_inc(S[f"nm{i}"], 1)
                pool.tensor_tensor(ve[i][:], mv[i][:, 1:2], const[:, C_EPS + i:C_EPS + i + 1], ALU.add).then_inc(S[f"ve{i}"], 1)
                done(pool, f"ve{i}", tile)
                pool.tensor_tensor(rstd[i][:], ve[i][:], minus_half, ALU.pow).then_inc(S[f"rstd{i}"], 1)
                if i in (1, 3):
                    done(pool, f"nm{i}", tile)
                    done(pool, f"rstd{i}", tile)
                    pool.tensor_tensor(offset[i][:], neg_mean[i][:], rstd[i][:], ALU.mult).then_inc(S[f"off{i}"], 1)

            def products(tile, part):
                t, p, n = tile
                product = products_of[part]
                pool.wait_ge(x_in[p], 64 * (n + 1))
                done(pool, f"dot{part}", tile, 1)
                pool.tensor_tensor(product[:], xx[p][:, 0, part * JR * D:(part + 1) * JR * D].rearrange("p (j d) -> p j d", j=JR),
                                   wproj[:].rearrange("p (a d) -> p a d", a=1).broadcast_to([P, JR, D]), ALU.mult).then_inc(S[f"prod{part}"], 1)
                done(pool, f"prod{part}", tile)
                pool.tensor_tensor(product[:, :, 0], product[:, :, 0], wproj_b[:].broadcast_to([P, JR]), ALU.add).then_inc(S[f"prod{part}b"], 1)

            def carry_state(tile):
                done(pool, "stated1", tile, 1)
                done(pool, "stated0", tile, 1)
                pool.tensor_tensor(carried[:], state[1 - tile[1]][:, :, CLIPS:P], decay[:], ALU.mult).then_inc(S["carriedd"], 1)

            def spread_weights(tile):
                done(pool, "weighted", tile)
                done(pool, "summed", tile, 1)
                pool.tensor_tensor(spread[:].rearrange("p s j b -> p (s j) b"),
                                   weight[:].rearrange("p (c a) -> p c a", a=1).broadcast_to([P, ST * JR, BL]),
                                   block_mask.rearrange("p (a b) -> p a b", a=1).broadcast_to([P, ST * JR, BL]),
                                   ALU.mult).then_inc(S["spreaded"], 1)

            def add_pos(tile):
                t, p, n = tile
                pool.wait_ge(pos_in[p], 32 * (n + 1))
                done(pool, "h1ed", tile, 1)
                pool.tensor_tensor(pos_b[:], pos[p][:], ln_b, ALU.add).then_inc(S["posb"], 1)

            def key_query(tile):
                done(pool, "qbed", tile)
                done(pool, "kbed", tile)
                done(pool, "scored", tile, 1)
                pool.tensor_tensor(kb[:], qb[:], kb[:], ALU.mult).then_inc(S["kqed"], 1)

            def value_bias(tile):
                done(pool, "vcopied", tile)
                pool.tensor_tensor(vb[:], vb[:], bv, ALU.add).then_inc(S["vbed"], 1)

            def weigh_value(tile):
                done(pool, "attned", tile)
                done(pool, "vbed", tile)
                done(pool, "uTed", tile, 1)
                pool.tensor_tensor(u[:].rearrange("p (h d) -> p h d", h=HEADS), vb[:].rearrange("p (h d) -> p h d", h=HEADS),
                                   attn[:].rearrange("p (h a) -> p h a", a=1).broadcast_to([P, HEADS, HD]), ALU.mult).then_inc(S["ued"], 1)

            def add_aug(tile):
                done(pool, "qsed", tile)
                done(pool, "auged", tile)
                done(pool, "woed", tile, 2)
                pool.tensor_tensor(oT[tile[1]][:], qs[:], aug[:], ALU.add).then_inc(S["oTed"], 1)

            def residual_bias(tile):
                done(pool, "h1ed", tile)
                done(pool, "h2ed", tile, 1)
                pool.tensor_tensor(h1b[:], h1[tile[1]][:], att_b, ALU.add).then_inc(S["h1bed"], 1)

            def period(A, B, C):
                if A:
                    products(A, 3)
                    products(A, 2)
                if B:
                    add_pos(B)
                if C:
                    add_aug(C)
                if B:
                    rstd_of(0, B)
                    rstd_of(1, B)
                if C:
                    rstd_of(2, C)
                    rstd_of(3, C)
                if A:
                    spread_weights(A)
                if B:
                    key_query(B)
                    carry_state(B)
                    value_bias(B)
                    residual_bias(B)
                    weigh_value(B)

            def routed(tile, first):
                t, p, n = tile
                done(pool, "acced", tile, 2)
                pool.tensor_tensor(pairs[p][:].rearrange("p s e g -> p s e g"),
                                   chosen[:, bass.ds(2 * t, 2), :].rearrange("p s (e a) -> p s e a", a=1).broadcast_to([P, 2, E, E]),
                                   segment[:, bass.ds(2 * t, 2), :].rearrange("p s (a g) -> p s a g", a=1).broadcast_to([P, 2, E, E]),
                                   ALU.mult).then_inc(S["paired"], 1)

            def setup():
                pool.wait_ge(setup_act, 1)
                pool.wait_ge(setup_dve, 1)
                pool.tensor_scalar(decay_cols[:], alpha_cols, 0.5, 0.5, ALU.mult, ALU.add).then_inc(setup_pool, 1)
                pool.tensor_scalar(keep_row, keep_row, -0.5, 0.5, ALU.mult, ALU.add).then_inc(setup_pool, 1)
                pool.wait_ge(setup_pool, 2)
                pool.tensor_copy(decay[:], decay_cols[:].rearrange("p (c a) -> p c a", a=1).broadcast_to([P, NC, CLIPS])).then_inc(setup_pool, 1)
                pool.tensor_tensor(bv, bv, keep_row, ALU.mult).then_inc(setup_pool, 1)
                pool.tensor_tensor(wv, wv, keep_row.rearrange("p (a n) -> p a n", a=1).broadcast_to([P, 2, CH]), ALU.mult).then_inc(setup_pool, 1)
                pool.wait_ge(setup_pool, SETUP_POOL)

            pool.wait_ge(early_in, 48)
            periods(pool, period, setup)
            pool.wait_ge(route, ROUTE_DONE)
            routed_tiles(pool, routed)

        @block.scalar
        def _(act):
            def squares(tile):
                t, p, n = tile
                act.wait_ge(x_in[p], 64 * (n + 1))
                done(act, "summed", tile, 2)
                act.activation(xx[p][:, 1, :], xx[p][:, 0, :], ACT.Square).then_inc(S["squared"], 1)

            def sum_products(tile, part):
                product = products_of[part]
                done(act, f"prod{part}b", tile)
                done(act, "shifted", tile, 1)
                for j in range(JR):
                    c = part * JR + j
                    last = act.activation(product[:, j, :], product[:, j, :], ACT.Copy, accum_out=logit[:, c:c + 1])
                last.then_inc(S[f"dot{part}"], 1)

            def exp_logits(tile):
                done(act, "shifted", tile)
                act.activation(expo[:], shifted[:], ACT.Exp).then_inc(S["exped"], 1)

            def mean_and_square(tile):
                done(act, "summed", tile)
                act.activation(mean_var[:, 0, :], bank[0][:, 0:D], ACT.Copy).then_inc(S["meaned"], 1)
                act.activation(mean_sq[:], bank[0][:, 0:D], ACT.Square).then_inc(S["msqed"], 1)

            def evacuate_stats(tile):
                p = tile[1]
                done(act, "statT", tile)
                done(act, "sprojed", tile, 2)
                act.activation(stats[p][:, 0:2, :].rearrange("p c n -> p (c n)"), bank[0][:, 0:2 * P], ACT.Copy)
                deviation = stats[p][:, 2:4, :].rearrange("p c n -> p (c n)")
                act.activation(deviation, bank[0][:, 2 * P:4 * P], ACT.Relu).then_inc(S["reluedv"], 1)
                done(act, "reluedv", tile)
                act.activation(deviation, deviation, ACT.Sqrt, bias=const[:, C_VAR:C_VAR + 1]).then_inc(S["statevac"], 1)

            def norm(i, dst, src, tile, name):
                done(act, f"off{i}", tile)
                act.activation(dst, src, ACT.Identity, bias=offset[i][:, 0:1], scale=rstd[i][:, 0:1]).then_inc(S[name], 1)

            def attention_in(tile):
                norm(1, a_in[:], h1[tile[1]][:], tile, "a_ined")

            def ffn_in(tile):
                norm(3, z[:], h2[:], tile, "zed")

            def evacuate_a(tile):
                done(act, "aTed", tile)
                act.activation(aT[:].rearrange("p c n -> p (c n)"), bank[4][:, 0:D], ACT.Copy).then_inc(S["aTevac"], 1)

            def copy_value(tile):
                done(act, "ved", tile)
                done(act, "ued", tile, 1)
                act.activation(vb[:], bank[4][:, :], ACT.Copy).then_inc(S["vcopied"], 1)

            def exp_scores(tile):
                done(act, "nmaxed", tile)
                act.activation(e_score[:], score[:], ACT.Exp, bias=neg_max[:, 0:1], accum_out=s_sum[:, 0:1]).then_inc(S["eed"], 1)

            def augment_tanh(tile):
                done(act, "qTed", tile)
                done(act, "oTed", tile, 1)
                for c in range(NC):
                    last = act.activation(aug[:, c, :], bank[5][:, c * P:(c + 1) * P], ACT.Tanh, scale=aug_cols[:, c:c + 1])
                last.then_inc(S["tanhed"], 1)

            def augment(tile):
                done(act, "tanhed", tile)
                act.activation(aug[:], aug[:], ACT.Copy, bias=0.5, scale=0.5).then_inc(S["auged"], 1)

            def evacuate_z(tile):
                t = tile[0]
                done(act, "zTed", tile)
                act.activation(zT[:].rearrange("p c n -> p (c n)"), bank[7][:, 0:D], ACT.Copy).then_inc(S["zTevac"], 1)
                act.activation(z_first[:, :, bass.ds(2 * t, 2)], bank[7][:, 0:D].rearrange("p (c n) -> p c n", c=2)[:, :, 0:P:CLIPS],
                               ACT.Copy).then_inc(S["zfirst"], 1)

            def gate_and_tanh(tile):
                t = tile[0]
                done(act, "ffned1", tile)
                act.activation(gate[:, bass.ds(t, 1), :].rearrange("p a e -> p (a e)"), bank[6][:, 0:E], ACT.Copy).then_inc(S["gated"], 1)
                done(act, "g1ed", tile, 1)
                act.activation(half_tanh[:], bank[6][:, E:E + D], ACT.Tanh, scale=0.5).then_inc(S["htanh"], 1)

            def evacuate_g(tile):
                done(act, "gTed", tile)
                act.activation(gT[:].rearrange("p c n -> p (c n)"), bank[6][:, 0:D], ACT.Copy).then_inc(S["gTevac"], 1)

            def period(A, B, C):
                if A:
                    sum_products(A, 2)
                    sum_products(A, 3)
                    exp_logits(A)
                if B:
                    attention_in(B)
                    evacuate_a(B)
                if A:
                    squares(A)
                if C:
                    ffn_in(C)
                    evacuate_z(C)
                if B:
                    copy_value(B)
                    exp_scores(B)
                if A:
                    mean_and_square(A)
                if C:
                    gate_and_tanh(C)
                if B:
                    augment_tanh(B)
                    augment(B)
                if C:
                    evacuate_g(C)
                if A:
                    evacuate_stats(A)

            def table_rows():
                done(act, "tabbed", tile_of(0, 0))
                for b in range(4):
                    last = act.activation(tab_rows[:, b // 2, (b % 2) * 512:(b % 2 + 1) * 512], bank[b][0:E, :], ACT.Copy)
                last.then_inc(S["tabrowed"], 1)

            def routed(tile, first):
                t, p, n = tile
                done(act, "pairTed", tile)
                done(act, "looked", tile, 2)
                act.activation(pairs_wT[p][:], bank[1 + p][:, 0:P], ACT.Copy).then_inc(S["pairTevac"], 1)
                done(act, "looked", tile)
                done(act, "r1ed", tile, 2)
                act.activation(r_tanh[p][:], psum[:, 4 + 2 * p:6 + 2 * p, 0:HID], ACT.Tanh, scale=0.5).then_inc(S["rtanhed"], 1)

            def setup():
                act.wait_ge(mats_in, 32)
                act.activation(alpha_cols, alpha_cols, ACT.Tanh, scale=0.5)
                act.activation(keep_row, keep_row, ACT.Tanh, scale=0.5).then_inc(setup_act, 1)
                act.activation(aug_cols, aug_cols, ACT.Copy, scale=0.5)
                act.activation(bk, bk, ACT.Copy, scale=HD ** -0.5)
                act.activation(wk, wk, ACT.Copy, scale=HD ** -0.5).then_inc(setup_act, 1)
                act.wait_ge(setup_act, 2)

            act.wait_ge(early_in, 48)
            periods(act, period, setup, between=table_rows)
            act.wait_ge(route, GATE_SHIFTED)
            act.activation(sc[:], sc[:], ACT.Exp).then_inc(gate_exp, 1)
            routed_tiles(act, routed)
            done(act, "acced", tile_of(0, TILES - 1))
            act.activation(hsum[:], bank[0][:, 0:HID], ACT.Copy).then_inc(hsummed, 1)
            act.wait_ge(hsumT_pe, 1)
            act.activation(hsumT0[:], bank[1][:, 0:PAIRS], ACT.Copy).then_inc(hsumT_act, 1)

        @block.tensor
        def _(pe):
            def logit_max_rows(tile):
                done(pe, "lmaxed", tile)
                pe.transpose(bank[1][0:ST, 0:P], logit_max[:], ident).then_inc(S["lmaxT"], 1)

            def block_max_cols(tile):
                done(pe, "bmaxed", tile)
                pe.matmul(bank[1][:, P:P + ST], block_max4[:].rearrange("s b q -> s (b q)"),
                          ident[0:ST, 0:ST], start=True, stop=True).then_inc(S["bmaxT"], 1)

            def block_sums(tile):
                done(pe, "esummed", tile)
                pe.matmul(bank[1][:, P:P + ST], same_block, expo_sum[:], start=True, stop=True).then_inc(S["denned"], 1)

            def weighted_sums(tile):
                p = tile[1]
                done(pe, "spreaded", tile)
                done(pe, "squared", tile)
                done(pe, "statevac", tile, 1)
                for j in range(JR):
                    for s in range(ST):
                        col = (s * JR + j) * D
                        last = pe.matmul(bank[0][s * BL:(s + 1) * BL, :], spread[:, s, j, :], xx[p][:, :, col:col + D],
                                         start=(j == 0), stop=(j == JR - 1), tile_position=(0, s * BL))
                last.then_inc(S["summed"], 1)

            def transpose_maxima(tile):
                done(pe, "maxed1", tile)
                done(pe, "maxq", tile, 1)
                for c in range(2):
                    for s in range(ST):
                        last = pe.transpose(bank[2 + c][:, s * P:(s + 1) * P], max1[:, s, c * P:(c + 1) * P], ident)
                last.then_inc(S["maxT"], 1)

            def transpose_stats(tile):
                done(pe, "varred", tile)
                for c in range(4):
                    last = pe.transpose(bank[0][:, c * P:(c + 1) * P], mean_var[:, c // 2, (c % 2) * P:(c % 2 + 1) * P], ident)
                last.then_inc(S["statT"], 1)

            def project_stats(tile):
                p = tile[1]
                done(pe, "statevac", tile)
                done(pe, "maxq", tile)
                done(pe, "stated1", tile, 1)
                for c in range(6):
                    last = pe.matmul(bank[4][:, 0:D], stats[p][:, c, :], sproj[:, c, :], start=(c == 0), stop=False)
                last = pe.matmul(bank[4][:, 0:D], ones[0:1, :], sproj_b[0:1, :], start=False, stop=True)
                last.then_inc(S["sprojed"], 1)

            def transpose_a(tile):
                done(pe, "a_ined", tile)
                for c in range(2):
                    last = pe.transpose(bank[4][:, c * P:(c + 1) * P], a_in[:, c * P:(c + 1) * P], ident)
                last.then_inc(S["aTed"], 1)

            def linear(to, w):
                for c in range(2):
                    last = pe.matmul(to, aT[:, c, :], w[:, c, :], start=(c == 0), stop=(c == 1))
                return last

            def query(tile):
                done(pe, "aTevac", tile)
                linear(bank[4][:, :], wq).then_inc(S["qed"], 1)

            def key(tile):
                done(pe, "aTevac", tile)
                done(pe, "qsed", tile, 1)
                linear(bank[5][:, :], wk).then_inc(S["ked"], 1)

            def value(tile):
                done(pe, "qbed", tile)
                linear(bank[4][:, :], wv).then_inc(S["ved"], 1)

            def transpose_q(tile):
                done(pe, "kbed", tile)
                for c in range(NC):
                    last = pe.transpose(bank[5][:, c * P:(c + 1) * P], qb[:, c * P:(c + 1) * P], ident)
                last.then_inc(S["qTed"], 1)

            def transpose_u(tile):
                done(pe, "ued", tile)
                for c in range(NC):
                    last = pe.transpose(bank[4][:, c * P:(c + 1) * P], u[:, c * P:(c + 1) * P], ident)
                last.then_inc(S["uTed"], 1)

            def project_out(tile):
                p = tile[1]
                done(pe, "oTed", tile)
                done(pe, "gTevac", tile, 1)
                for c in range(NC):
                    last = pe.matmul(bank[6][:, 0:D], oT[p][:, c, :], wo[:, c, :], start=(c == 0), stop=False)
                last = pe.matmul(bank[6][:, 0:D], ones[0:1, :], bo[0:1, :], start=False, stop=True)
                last.then_inc(S["woed"], 1)

            def transpose_z(tile):
                done(pe, "zed", tile)
                done(pe, "h3ed", tile, 1)
                for c in range(2):
                    last = pe.transpose(bank[7][:, c * P:(c + 1) * P], z[:, c * P:(c + 1) * P], ident)
                last.then_inc(S["zTed"], 1)

            def ffn_up1(tile):
                done(pe, "zTevac", tile)
                for c in range(2):
                    last = pe.matmul(bank[6][:, 0:E + D], zT[:, c, :], gate_up1[:, c, :], start=(c == 0), stop=(c == 1))
                last.then_inc(S["ffned1"], 1)

            def ffn_up3(tile):
                done(pe, "zfirst", tile)
                for c in range(2):
                    last = pe.matmul(bank[7][:, 0:D], zT[:, c, :], up3[:, c, :], start=(c == 0), stop=(c == 1))
                last.then_inc(S["ffned3"], 1)

            def transpose_g(tile):
                done(pe, "g2ed", tile)
                for c in range(2):
                    last = pe.transpose(bank[6][:, c * P:(c + 1) * P], g2[:, c * P:(c + 1) * P], ident)
                last.then_inc(S["gTed"], 1)

            def ffn_down(tile):
                done(pe, "gTevac", tile)
                for c in range(2):
                    last = pe.matmul(bank[7][:, 0:D], gT[:, c, :], down[:, c, :], start=(c == 0), stop=(c == 1))
                last.then_inc(S["downed"], 1)

            def period(A, B, C):
                if B:
                    project_stats(B)
                if A:
                    logit_max_rows(A)
                    block_max_cols(A)
                if C:
                    project_out(C)
                if B:
                    transpose_a(B)
                if A:
                    block_sums(A)
                if B:
                    query(B)
                    key(B)
                    value(B)
                if C:
                    transpose_z(C)
                if A:
                    weighted_sums(A)
                if C:
                    ffn_up1(C)
                if B:
                    transpose_q(B)
                if C:
                    ffn_up3(C)
                if B:
                    transpose_u(B)
                if C:
                    transpose_g(C)
                if A:
                    transpose_stats(A)
                if C:
                    ffn_down(C)
                if A:
                    transpose_maxima(A)

            def table():
                pe.wait_ge(experts_in, 16)
                done(pe, "zfirst", tile_of(0, E // 2 - 1))
                for b in range(4):
                    w = (w1, w3)[b // 2]
                    for c in range(2):
                        last = pe.matmul(bank[b][0:E, :], z_first[:, c, 0:E], w[:, c, (b % 2) * 4:(b % 2 + 1) * 4, :],
                                         start=(c == 0), stop=(c == 1))
                last.then_inc(S["tabbed"], 1)

            def routed(tile, first):
                t, p, n = tile
                done(pe, "pairwed", tile)
                done(pe, "pairTevac", tile, 2)
                pe.transpose(bank[1 + p][:, 0:P], pairs_w[p][:].rearrange("p s e g -> p (s e g)"), ident).then_inc(S["pairTed"], 1)
                done(pe, "pairTevac", tile)
                done(pe, "r2ed", tile, 2)
                for s in range(2):
                    last = pe.matmul(bank[4 + 2 * p + s][:, 0:2 * HID], pairs_wT[p][s * PAIRS:(s + 1) * PAIRS, :],
                                     tab[s * PAIRS:(s + 1) * PAIRS, :, :].rearrange("p k n -> p (k n)"), start=True, stop=True)
                last.then_inc(S["looked"], 1)
                done(pe, "r2ed", tile)
                done(pe, "paired", tile)
                for s in range(2):
                    last = pe.matmul(bank[0][s * PAIRS:(s + 1) * PAIRS, 0:HID], pairs[p][:, s].rearrange("p e g -> p (e g)"),
                                     r2[p][:, s, :], start=first, stop=True, skip_group_check=True)
                last.then_inc(S["acced"], 1)

            def setup():
                pe.wait_ge(mats_in, 32)
                pe.wait_ge(setup_act, 2)
                pe.wait_ge(setup_pool, SETUP_POOL)

            pe.wait_ge(early_in, 48)
            periods(pe, period, setup, between=table)
            pe.wait_ge(route, COUNT_READY)
            pe.matmul(bank[3][:, 0:E], ones, mine[:], start=True, stop=True).then_inc(counted, 1)
            pe.wait_ge(tab_in, 64)
            done(pe, "tabrowed", tile_of(0, 0))
            routed_tiles(pe, routed)
            pe.wait_ge(hsummed, 1)
            pe.transpose(bank[1][:, 0:P], hsum[:], ident).then_inc(hsumT_pe, 1)
            pe.wait_ge(experts_in, 32)
            pe.wait_ge(rouT, 1)
            for g in range(E):
                last = pe.matmul(bank[3][0:E, 0:D], hsumT[:, g:PAIRS:E], w2[:, g, :], start=(g == 0), stop=(g == E - 1))
            last.then_inc(final_pe, 1)

        @block.vector
        def _(dve):
            def dots(tile, part):
                t, p, n = tile
                if part == 0:
                    dve.wait_ge(x_in[p], 64 * (n + 1))
                done(dve, f"dot{1 - part}", tile, 1 - part)
                for c in range(part * JR, (part + 1) * JR):
                    last = dve.tensor_tensor_reduce(out=product[:, c % JR, :], in0=xx[p][:, 0, c * D:(c + 1) * D], in1=wproj[:],
                                                    scale=1.0, scalar=wproj_b[:, 0:1], op0=ALU.mult, op1=ALU.add,
                                                    accum_out=logit[:, c:c + 1])
                last.then_inc(S[f"dot{part}"], 1)

            def maxima2(tile):
                p = tile[1]
                dve.wait_ge(x_in[p], 64 * (tile[2] + 1))
                rows = xx[p][:, 0, :].rearrange("p (s n) -> p s n", s=ST)
                dve.tensor_tensor(max2[:], rows[:, :, 0:2 * D], rows[:, :, 2 * D:4 * D], ALU.max).then_inc(S["maxed2"], 1)

            def maxima1(tile):
                done(dve, "maxed2", tile)
                done(dve, "maxT", tile, 1)
                dve.tensor_tensor(max1[:], max2[:, :, 0:D], max2[:, :, D:2 * D], ALU.max).then_inc(S["maxed1"], 1)

            def maxima_of_blocks(tile):
                done(dve, "maxT", tile)
                done(dve, "sprojed", tile, 2)
                dve.tensor_reduce(stats[tile[1]][:, 4:6, :], psum[:, 2:4, :].rearrange("p c (n q) -> p c n q", q=Q),
                                  AX.X, ALU.max).then_inc(S["maxq"], 1)

            def logit_max_of_rows(tile):
                for part in range(1, ST):
                    done(dve, f"dot{part}", tile)
                dve.tensor_reduce(logit_max[:], logit[:].rearrange("p (s j) -> p s j", j=JR), AX.X, ALU.max).then_inc(S["lmaxed"], 1)

            def logit_max_of_blocks(tile):
                done(dve, "lmaxT", tile)
                dve.tensor_reduce(block_max[:], bank[1][0:ST, 0:P].rearrange("s (b q) -> s b q", q=Q), AX.X, ALU.max).then_inc(S["bmaxed0"], 1)
                done(dve, "bmaxed0", tile)
                dve.tensor_copy(block_max4[:], block_max[:].rearrange("s (b a) -> s b a", a=1).broadcast_to([ST, BL, Q])).then_inc(S["bmaxed"], 1)

            def per_block(ap):
                return ap.rearrange("p (s a) -> p s a", a=1).broadcast_to([P, ST, JR])

            def shift_logits(tile):
                done(dve, "bmaxT", tile)
                dve.tensor_tensor(shifted[:].rearrange("p (s j) -> p s j", j=JR), logit[:].rearrange("p (s j) -> p s j", j=JR),
                                  per_block(bank[1][:, P:P + ST]), ALU.subtract).then_inc(S["shifted"], 1)

            def sum_expo(tile):
                done(dve, "exped", tile)
                dve.tensor_reduce(expo_sum[:], expo[:].rearrange("p (s j) -> p s j", j=JR), AX.X, ALU.add).then_inc(S["esummed"], 1)

            def normalise(tile):
                done(dve, "denned", tile)
                dve.reciprocal(inv_sum[:], bank[1][:, P:P + ST]).then_inc(S["rdenned"], 1)
                done(dve, "rdenned", tile)
                dve.tensor_tensor(weight[:].rearrange("p (s j) -> p s j", j=JR), expo[:].rearrange("p (s j) -> p s j", j=JR),
                                  per_block(inv_sum[:]), ALU.mult).then_inc(S["weighted"], 1)

            def variance(tile):
                done(dve, "msqed", tile)
                dve.tensor_tensor(mean_var[:, 1, :], bank[0][:, D:2 * D], mean_sq[:], ALU.subtract).then_inc(S["varred"], 1)

            def norm_stats(i, src, tile, ready):
                done(dve, ready, tile)
                dve.bn_stats(bn[i][:], src).then_inc(S[f"bn{i}"], 1)
                done(dve, f"bn{i}", tile)

            def norm_mean(i, tile):
                dve.bn_aggr(mv[i][:], bn[i][:]).then_inc(S[f"mv{i}"], 1)

            def token(tile):
                norm_stats(0, bank[4][:, 0:D], tile, "sprojed")

            def token_scale(tile):
                done(dve, "mv0", tile)
                done(dve, "h1ed", tile, 1)
                dve.scalar_tensor_tensor(out=h0[:], in0=bank[4][:, 0:D], scalar=mv[0][:, 0:1], in1=ln_g, op0=ALU.subtract, op1=ALU.mult).then_inc(S["h0ced"], 1)

            def token_out(tile):
                p = tile[1]
                done(dve, "rstd0", tile)
                done(dve, "posb", tile)
                done(dve, "h0ced", tile)
                done(dve, "h1bed", tile, 2)
                dve.scalar_tensor_tensor(out=h1[p][:], in0=h0[:], scalar=rstd[0][:, 0:1], in1=pos_b[:], op0=ALU.mult, op1=ALU.add).then_inc(S["h1ed"], 1)
                norm_stats(1, h1[p][:], tile, "h1ed")

            def query_bias(tile):
                done(dve, "qed", tile)
                done(dve, "qTed", tile, 1)
                done(dve, "kqed", tile, 1)
                dve.tensor_tensor(qb[:], bank[4][:, :], bq, ALU.add).then_inc(S["qbed"], 1)

            def key_bias(tile):
                done(dve, "scored", tile, 1)
                done(dve, "ked", tile)
                dve.tensor_tensor(kb[:], bank[5][:, :], bk, ALU.add).then_inc(S["kbed"], 1)

            def scores(tile):
                done(dve, "kqed", tile)
                dve.tensor_reduce(score[:], kb[:].rearrange("p (h d) -> p h d", h=HEADS), AX.X, ALU.add).then_inc(S["scored"], 1)
                done(dve, "scored", tile)
                dve.tensor_reduce(neg_max[:], score[:], AX.X, ALU.max, negate=True).then_inc(S["nmaxed"], 1)

            def head_softmax(tile):
                done(dve, "eed", tile)
                dve.reciprocal(s_inv[:], s_sum[:]).then_inc(S["sinved"], 1)
                done(dve, "sinved", tile)
                dve.tensor_scalar(attn[:], e_score[:], s_inv[:, 0:1], None, ALU.mult).then_inc(S["attned"], 1)

            def advance_state(tile):
                now, u_now = state[tile[1]], bank[4][:, :].rearrange("p (c n) -> p c n", c=NC)
                done(dve, "uTed", tile)
                done(dve, "carriedd", tile)
                dve.tensor_tensor(now[:, :, 0:CLIPS], carried[:], u_now[:, :, 0:CLIPS], ALU.add).then_inc(S["stated0"], 1)
                done(dve, "stated0", tile)
                dve.tensor_tensor(decayed[:], now[:, :, 0:CLIPS], decay[:], ALU.mult).then_inc(S["decayedd"], 1)
                done(dve, "decayedd", tile)
                dve.tensor_tensor(now[:, :, CLIPS:P], decayed[:], u_now[:, :, CLIPS:P], ALU.add).then_inc(S["stated1"], 1)

            def query_state(tile):
                done(dve, "stated1", tile)
                done(dve, "tanhed", tile)
                done(dve, "oTed", tile, 1)
                dve.tensor_tensor(qs[:], bank[5][:, :].rearrange("p (c n) -> p c n", c=NC), state[tile[1]][:], ALU.mult).then_inc(S["qsed"], 1)

            def attention_out(tile):
                norm_stats(2, bank[6][:, 0:D], tile, "woed")

            def attention_scale(tile):
                done(dve, "mv2", tile)
                done(dve, "h2ed", tile, 1)
                dve.scalar_tensor_tensor(out=o_raw[:], in0=bank[6][:, 0:D], scalar=mv[2][:, 0:1], in1=att_g, op0=ALU.subtract, op1=ALU.mult).then_inc(S["oced"], 1)

            def residual(tile):
                done(dve, "rstd2", tile)
                done(dve, "h1bed", tile)
                done(dve, "oced", tile)
                dve.scalar_tensor_tensor(out=h2[:], in0=o_raw[:], scalar=rstd[2][:, 0:1], in1=h1b[:], op0=ALU.mult, op1=ALU.add).then_inc(S["h2ed"], 1)
                norm_stats(3, h2[:], tile, "h2ed")

            def silu_a(tile):
                done(dve, "htanh", tile)
                dve.scalar_tensor_tensor(out=half_tanh[:], in0=half_tanh[:], scalar=1.0, in1=bank[6][:, E:E + D], op0=ALU.add, op1=ALU.mult).then_inc(S["g1ed"], 1)

            def silu_b(tile):
                done(dve, "ffned3", tile)
                done(dve, "g1ed", tile)
                dve.scalar_tensor_tensor(out=g2[:], in0=half_tanh[:], scalar=0.5, in1=bank[7][:, 0:D], op0=ALU.mult, op1=ALU.mult).then_inc(S["g2ed"], 1)

            def result(tile):
                t, p, n = tile
                done(dve, "downed", tile)
                if not (isinstance(n, int) and n < 1):
                    dve.wait_ge(stored[p], 32 * n)
                dve.tensor_tensor(h3[p][:], bank[7][:, 0:D], h2[:], ALU.add).then_inc(S["h3ed"], 1)

            def period(A, B, C):
                if B:
                    maxima_of_blocks(B)
                if A:
                    dots(A, 0)
                    dots(A, 1)
                if B:
                    token(B)
                if A:
                    logit_max_of_rows(A)
                if B:
                    norm_mean(0, B)
                    token_scale(B)
                if A:
                    logit_max_of_blocks(A)
                if B:
                    token_out(B)
                if A:
                    shift_logits(A)
                if B:
                    norm_mean(1, B)
                if C:
                    attention_out(C)
                if A:
                    sum_expo(A)
                if C:
                    norm_mean(2, C)
                    attention_scale(C)
                    residual(C)
                if A:
                    normalise(A)
                if B:
                    query_bias(B)
                if C:
                    norm_mean(3, C)
                if A:
                    maxima2(A)
                if B:
                    key_bias(B)
                    scores(B)
                    head_softmax(B)
                if A:
                    maxima1(A)
                    variance(A)
                if C:
                    silu_a(C)
                    silu_b(C)
                if B:
                    advance_state(B)
                if C:
                    result(C)
                if B:
                    query_state(B)

            def routed(tile, first):
                t, p, n = tile
                done(dve, "pairTed", tile, 2)
                dve.tensor_tensor(pairs_w[p][:],
                                  chosen_w[:, bass.ds(2 * t, 2), :].rearrange("p s (e a) -> p s e a", a=1).broadcast_to([P, 2, E, E]),
                                  segment[:, bass.ds(2 * t, 2), :].rearrange("p s (a g) -> p s a g", a=1).broadcast_to([P, 2, E, E]),
                                  ALU.mult).then_inc(S["pairwed"], 1)
                done(dve, "rtanhed", tile)
                ab = psum[:, 4 + 2 * p:6 + 2 * p, 0:2 * HID].rearrange("p s (k n) -> p k s n", k=2)
                dve.scalar_tensor_tensor(out=r1[p][:], in0=r_tanh[p][:], scalar=1.0, in1=ab[:, 0], op0=ALU.add, op1=ALU.mult).then_inc(S["r1ed"], 1)
                done(dve, "r1ed", tile)
                done(dve, "acced", tile, 2)
                dve.scalar_tensor_tensor(out=r2[p][:], in0=r1[p][:], scalar=0.5, in1=ab[:, 1], op0=ALU.mult, op1=ALU.mult).then_inc(S["r2ed"], 1)

            def setup():
                dve.wait_ge(mats_in, 32)
                dve.wait_ge(setup_act, 2)
                dve.wait_ge(setup_pool, SETUP_POOL)

            dve.memset(state[1][:], 0.0).then_inc(setup_dve, 1)
            dve.wait_ge(early_in, 48)
            periods(dve, period, setup)

            steps = [0]

            def link(instruction):
                steps[0] += 1
                instruction.then_inc(route, 1)
                dve.wait_ge(route, steps[0])

            def cols(ap, n):
                return ap.rearrange("p (t a) -> p t a", a=1).broadcast_to([P, TILES, n])

            def ranks(out_rank, values, n, before):
                gt = cmp_gt[:, 0:TILES * n * n].rearrange("p (t a b) -> p t a b", a=n, b=n)
                ge = cmp_ge[:, 0:TILES * n * n].rearrange("p (t a b) -> p t a b", a=n, b=n)
                other = values.rearrange("p t (a b) -> p t a b", a=1).broadcast_to([P, TILES, n, n])
                own = values.rearrange("p t (a b) -> p t a b", b=1).broadcast_to([P, TILES, n, n])
                dve.tensor_tensor(gt, other, own, ALU.is_gt)
                link(dve.tensor_tensor(ge, other, own, ALU.is_ge))
                link(dve.tensor_tensor(ge, ge, before.rearrange("p (z a b) -> p z a b", z=1, a=n).broadcast_to([P, TILES, n, n]), ALU.mult))
                link(dve.tensor_tensor(gt, gt, ge, ALU.max))
                link(dve.tensor_reduce(out_rank, gt, AX.X, ALU.add))

            done(dve, "gated", tile_of(0, TILES - 1))
            link(dve.tensor_reduce(t1[:], gate[:], AX.X, ALU.max))
            link(dve.tensor_tensor(sc[:], gate[:], cols(t1[:], E), ALU.subtract))
            assert steps[0] == GATE_SHIFTED
            dve.wait_ge(gate_exp, 1)
            link(dve.tensor_reduce(t1[:], sc[:], AX.X, ALU.add))
            link(dve.reciprocal(t1[:], t1[:]))
            link(dve.tensor_tensor(sc[:], sc[:], cols(t1[:], E), ALU.mult))
            link(dve.tensor_tensor(s2[:], sc[:], ebias.rearrange("p (a e) -> p a e", a=1).broadcast_to([P, TILES, E]), ALU.add))
            link(dve.tensor_reduce(gsum[:], s2[:].rearrange("p t (g m) -> p t g m", m=E // G), AX.X, ALU.add))
            ranks(grank[:], gsum[:], G, const[:, C_LT4:C_LT4 + 16])
            link(dve.tensor_scalar(grank[:], grank[:], 2.0, -1e30, ALU.is_ge, ALU.mult))
            link(dve.tensor_tensor(s3[:].rearrange("p t (g m) -> p t g m", m=E // G), s2[:].rearrange("p t (g m) -> p t g m", m=E // G),
                                   grank[:].rearrange("p t (g a) -> p t g a", a=1).broadcast_to([P, TILES, G, E // G]), ALU.add))
            ranks(rank[:], s3[:], E, const[:, C_LT8:C_LT8 + 64])
            by_slot = chosen[:].rearrange("p (t s) e -> p t s e", s=2)
            for s in range(2):
                last = dve.tensor_scalar(by_slot[:, :, s, :], rank[:], float(s), None, ALU.is_equal)
            link(last)
            link(dve.memset(chosen[CLIPS:P, 2 * TILES - 2:2 * TILES, :], 0.0))
            link(dve.tensor_reduce(mine[:], chosen[:].rearrange("p n e -> p e n"), AX.X, ALU.add))
            assert steps[0] == COUNT_READY
            for s in range(2):
                last = dve.tensor_tensor(chosen_w[:].rearrange("p (t s) e -> p t s e", s=2)[:, :, s, :], by_slot[:, :, s, :], sc[:], ALU.mult)
            link(last)
            dve.wait_ge(counted, 1)
            link(dve.tensor_copy(count[:], bank[3][:, 0:E]))
            link(dve.tensor_tensor_scan(seg_end[:], ones[:, 0:E], count[:], 0.0, ALU.mult, ALU.add))
            link(dve.tensor_tensor(seg_start[:], seg_end[:], count[:], ALU.subtract))
            position = const[:, C_POS:C_POS + 2 * TILES].rearrange("p (n a) -> p n a", a=1).broadcast_to([P, 2 * TILES, E])
            bounds = lambda ap: ap.rearrange("p (a e) -> p a e", a=1).broadcast_to([P, 2 * TILES, E])
            dve.tensor_tensor(segment[:], position, bounds(seg_start[:]), ALU.is_ge)
            link(dve.tensor_tensor(seg_hi[:], position, bounds(seg_end[:]), ALU.is_lt))
            link(dve.tensor_tensor(segment[:], segment[:], seg_hi[:], ALU.mult))
            assert steps[0] == ROUTE_DONE
            routed_tiles(dve, routed)
            dve.wait_ge(hsumT_act, 1)
            dve.tensor_tensor(hsumT[:], bank[1][:, PAIRS:2 * PAIRS], hsumT0[:], ALU.add).then_inc(rouT, 1)
            dve.wait_ge(final_pe, 1)
            dve.wait_ge(first8_in, 16)
            dve.tensor_tensor(first8_out[:], bank[3][0:E, 0:D], first8[:], ALU.add).then_inc(final_dve, 1)


SETUP_POOL = 5
GATE_SHIFTED, COUNT_READY, ROUTE_DONE = 2, 20, 26

SHAPE = (CLIPS, NBLK, D)


def kernel(**inputs):
    import concourse.bacc as bacc
    from concourse.bass_utils import run_bass_kernel_spmd

    arrays = {n: np.ascontiguousarray(v) for n, v in inputs.items()}
    on_partitions = lambda w: w.reshape(-1, P, w.shape[-1]).transpose(1, 0, 2).reshape(P, -1)
    take = arrays.pop
    sw1, sw2, sw3 = (take("L0_ffn_" + n).T for n in ("sw1", "sw2", "sw3"))
    gate_sw1 = np.concatenate([take("L0_ffn_w_gate").T, sw1], axis=1)
    columns = lambda v: v.reshape(NC, P).T
    arrays["mats"] = np.concatenate(
        [on_partitions(w) for w in (take("L0_tok_s_proj_w"), take("L0_attn_Wq"), take("L0_attn_Wk"), take("L0_attn_Wv"), take("L0_attn_Wo"),
                                    gate_sw1, sw3, sw2)]
        + [columns(arrays["L0_attn_alpha"]), columns(take("L0_attn_aug_param"))], axis=1)
    arrays["rows"] = np.concatenate([take(n).reshape(1, -1) for n in (
        "L0_tok_s_proj_b", "L0_tok_ln_g", "L0_tok_ln_b", "L0_attn_bo", "L0_attn_ln_scale", "L0_attn_ln_bias",
        "L0_attn_bq", "L0_attn_bk", "L0_attn_bv", "L0_attn_alpha", "L0_ffn_expert_bias")], axis=1)
    arrays["experts"] = np.concatenate(
        [take("L0_ffn_" + n).reshape(E, 2, P, HID).transpose(2, 1, 0, 3).reshape(P, -1) for n in ("w1", "w3")]
        + [take("L0_ffn_w2").transpose(1, 0, 2).reshape(P, -1)], axis=1)
    arrays["const"] = constants()
    arrays["zeros"] = np.zeros((P, JR * D), np.float32)
    nc = bacc.Bacc("TRN2", target_bir_lowering=False, num_devices=1)
    aps = {n: nc.dram_tensor("in_" + n, v.shape, mybir.dt.from_np(v.dtype), kind="ExternalInput").ap() for n, v in arrays.items()}
    out = nc.dram_tensor("tower_out", SHAPE, F32, kind="ExternalOutput").ap()
    audio_tower(nc, aps, out)
    r = run_bass_kernel_spmd(nc, [{"in_" + n: v for n, v in arrays.items()}], core_ids=[0])
    return r.results[0]["tower_out"]
```

```python
from contextlib import ExitStack

import numpy as np

import concourse.bass as bass
from concourse import mybir

F32 = mybir.dt.float32
ALU = mybir.AluOpType
ACT = mybir.ActivationFunctionType
AX = mybir.AxisListType

P = 128
CLIPS, ROWS, D = 64, 750, 256
BLOCK = 16
NBLK = -(-ROWS // BLOCK)
TILES = -(-NBLK // 2)
ST = 4
JR = 4
Q = BLOCK // JR
BL = P // Q
HEADS, HD = 8, 64
CH = HEADS * HD
NC = CH // P
E, HID = 8, 128
G = 4
PAIRS = E * E
POS_ROWS = NBLK + 1
LN_TOK, LN_ATT, LN_H, VAR_EPS = 1e-5, 1e-6, 1e-5, 1e-8

C_ID, C_ONES, C_BLK, C_MASK, C_HALF = 0, 128, 256, 384, 416
C_EPS = C_HALF + 1
C_VAR, C_NEG = C_EPS + 4, C_EPS + 5
C_POS = C_NEG + 1
C_DESC = C_POS + 2 * TILES
C_LT4 = C_DESC + E
C_SEL = C_LT4 + G * G
C_END = C_SEL + PAIRS


MATS = [(6, D), (2, CH), (2, CH), (2, CH), (NC, D), (2, E + D), (2, D), (2, D), (NC,), (NC,)]
ROWVECS = [D] * 6 + [CH] * 4 + [E]


def constants():
    p = np.arange(P)
    c = np.zeros((P, C_END), np.float32)
    c[:, C_ID:C_ID + P] = np.eye(P)
    c[:, C_ONES:C_ONES + P] = 1.0
    c[:, C_BLK:C_BLK + P] = p[:, None] // Q == p[None, :] // Q
    c[:, C_MASK:C_MASK + BL] = p[:, None] // Q == np.arange(BL)[None, :]
    c[:, C_HALF] = -0.5
    c[:, C_EPS:C_EPS + 4] = (LN_TOK, LN_H, LN_ATT, LN_H)
    c[:, C_VAR], c[:, C_NEG] = VAR_EPS, -1.0
    t = np.arange(TILES)[None, :, None]
    s = np.arange(2)[None, None, :]
    token = (p[:, None, None] % CLIPS) * NBLK + 2 * t + p[:, None, None] // CLIPS
    c[:, C_POS:C_POS + 2 * TILES] = (2 * token + s).reshape(P, -1)
    c[:, C_DESC:C_DESC + E] = E - np.arange(E)
    c[:, C_LT4:C_LT4 + G * G] = (np.arange(G)[None, :] < np.arange(G)[:, None]).reshape(-1)
    c[:, C_SEL:C_SEL + PAIRS] = p[:, None] % PAIRS == np.arange(PAIRS)[None, :]
    return c


def audio_tower(nc, a, out):
    x = a["x"]
    with ExitStack() as ctx:
        def sb(name, *shape):
            return ctx.enter_context(nc.sbuf_tensor(name, list(shape), F32))

        def sem(name):
            return ctx.enter_context(nc.semaphore(name))

        const = sb("const", P, C_END)
        ident = const[:, C_ID:C_ID + P]
        ones = const[:, C_ONES:C_ONES + P]
        same_block = const[:, C_BLK:C_BLK + P]
        block_mask = const[:, C_MASK:C_MASK + BL]
        minus_half = const[:, C_HALF:C_HALF + 1]
        wproj, wproj_b = sb("wproj", P, D), sb("wproj_b", P, 1)
        zeros = a["zeros"]

        def views(tensor, parts):
            at, out = 0, []
            for shape in parts:
                n = int(np.prod(shape))
                part = tensor[:, at:at + n]
                if len(shape) > 1:
                    dims = " ".join("abc"[:len(shape)])
                    part = part.rearrange(f"p ({dims}) -> p {dims}", **dict(zip("abc", shape)))
                out.append(part)
                at += n
            return out

        mats = sb("mats", P, sum(int(np.prod(m)) for m in MATS))
        sproj, wq, wk, wv, wo, gate_up1, up3, down, alpha_cols, aug_cols = views(mats, MATS)
        rows = sb("rows", P, sum(ROWVECS))
        sproj_b, ln_g, ln_b, bo, att_g, att_b, bq, bk, bv, keep_row, ebias = views(rows, [(n,) for n in ROWVECS])
        experts = sb("experts", P, 2 * E * D)
        w1, w3 = views(experts, [(2, E, HID), (2, E, HID)])
        decay_cols = sb("decay_cols", P, NC)
        decay = sb("decay", P, NC, CLIPS)

        xx = [sb(f"xx{i}", P, 2, ST * JR * D) for i in range(2)]
        product = sb("product", P, JR, D)
        products_of = {part: sb(f"products{part}", P, JR, D) for part in (2, 3)}
        max2, max1 = sb("max2", P, ST, 2 * D), sb("max1", P, ST, D)
        logit = sb("logit", P, ST * JR)
        logit_max, block_max, block_max4 = sb("logit_max", P, ST), sb("block_max", ST, BL), sb("block_max4", ST, BL, Q)
        shifted, expo, weight = sb("shifted", P, ST * JR), sb("expo", P, ST * JR), sb("weight", P, ST * JR)
        expo_sum, inv_sum = sb("expo_sum", P, ST), sb("inv_sum", P, ST)
        spread = sb("spread", P, ST, JR, BL)
        mean_var, mean_sq = sb("mean_var", P, 2, D), sb("mean_sq", P, D)
        stats = [sb(f"stats{i}", P, 6, P) for i in range(2)]
        pos = [sb(f"pos{i}", P, D) for i in range(2)]
        pos_b = sb("pos_b", P, D)
        h0 = sb("h0", P, D)
        bn = [sb(f"bn{i}", P, 6) for i in range(4)]
        mv = [sb(f"mv{i}", P, 2) for i in range(4)]
        neg_mean = [sb(f"neg_mean{i}", P, 1) for i in range(4)]
        offset = [sb(f"offset{i}", P, 1) for i in range(4)]
        ve = [sb(f"ve{i}", P, 1) for i in range(4)]
        rstd = [sb(f"rstd{i}", P, 1) for i in range(4)]
        h1 = [sb(f"h1_{i}", P, D) for i in range(2)]
        a_in, aT = sb("a_in", P, D), sb("aT", P, 2, P)
        qb, kb, vb = sb("qb", P, CH), sb("kb", P, CH), sb("vb", P, CH)
        score, neg_max, e_score = sb("score", P, HEADS), sb("neg_max", P, 1), sb("e_score", P, HEADS)
        s_sum, s_inv, attn = sb("s_sum", P, 1), sb("s_inv", P, 1), sb("attn", P, HEADS)
        u = sb("u", P, CH)
        carried = sb("carried", P, NC, CLIPS)
        decayed = sb("decayed", P, NC, CLIPS)
        aug = sb("aug", P, NC, P)
        state = [sb(f"state{i}", P, NC, P) for i in range(2)]
        qs = sb("qs", P, NC, P)
        oT = [sb(f"oT{i}", P, NC, P) for i in range(2)]
        h1b, o_raw, h2 = sb("h1b", P, D), sb("o_raw", P, D), sb("h2", P, D)
        z, zT = sb("z", P, D), sb("zT", P, 2, P)
        z_first = sb("z_first", P, 2, 2 * TILES)
        gate = sb("gate", P, TILES, E)
        half_tanh, g2, gT = sb("half_tanh", P, D), sb("g2", P, D), sb("gT", P, 2, P)
        h3 = [sb(f"h3_{i}", P, D) for i in range(2)]

        spares = [b[:].rearrange("p k n -> p (k n)") for b in xx]
        used = [0]

        def carve(name, *shape):
            size = int(np.prod(shape[1:]))
            if used[0] + size > 2 * ST * JR * D:
                spares.pop(0)
                used[0] = 0
            part = spares[0][0:shape[0], used[0]:used[0] + size]
            used[0] += size
            if len(shape) == 2:
                return part
            dims = " ".join("abc"[:len(shape) - 1])
            return part.rearrange(f"p ({dims}) -> p {dims}", **dict(zip("abc", shape[1:])))

        w2, first8, first8_out = carve("w2", P, E, D), carve("first8", E, D), carve("first8_out", E, D)
        sc, s2 = carve("sc", P, TILES, E), carve("s2", P, TILES, E)
        t1, gsum, grank = carve("t1", P, TILES), carve("gsum", P, TILES, G), carve("grank", P, TILES, G)
        cmp_gt, cmp_ge = carve("cmp_gt", P, TILES, G, G), carve("cmp_ge", P, TILES, G, G)
        equal, best = carve("equal", P, TILES, E), carve("best", P, TILES)
        chosen, chosen_w, chosen_w2, segment, seg_hi = (
            carve(n, P, 2 * TILES, E) for n in ("chosen", "chosen_w", "chosen_w2", "segment", "seg_hi"))
        mine, count, seg_end, seg_start = (carve(n, P, E) for n in ("mine", "count", "seg_end", "seg_start"))
        tab_rows = carve("tab_rows", E, 2, E * HID)
        tab, tab_diag, tab_13 = carve("tab", P, 2, HID), carve("tab_diag", P, 2, HID), carve("tab_13", P, HID)
        pairs_w, pairs_w2 = ([carve(f"{n}{i}", P, 2, E, E) for i in range(2)] for n in ("pairs_w", "pairs_w2"))
        pairs_wT = [carve(f"pairs_wT{i}", P, P) for i in range(2)]
        r_tanh = [carve(f"r_tanh{i}", P, 2, HID + 1) for i in range(2)]
        w_sum, hsum, hsumT = carve("w_sum", P, 1), carve("hsum", P, HID), carve("hsumT", P, PAIRS)

        psum = ctx.enter_context(nc.psum_tensor("psum", [P, 8, 512], F32))
        bank = [psum[:, i, :] for i in range(8)]

        early_in, mats_in, experts_in = sem("early_in"), sem("mats_in"), sem("experts_in")
        setup_act, setup_dve, setup_pool = sem("setup_act"), sem("setup_dve"), sem("setup_pool")
        x_in = [sem(f"x_in{i}") for i in range(2)]
        pos_in = [sem(f"pos_in{i}") for i in range(2)]
        stored = [sem(f"stored{i}") for i in range(2)]
        names = """prod2 prod2b prod3 prod3b dot0 dot1 dot2 dot3 maxed2 maxed1 squared lmaxed lmaxT bmaxed0 bmaxed bmaxT shifted exped esummed denned rdenned
            weighted spreaded summed maxT maxq meaned msqed varred reluedv statT statevac
            sprojed bn0 mv0 ve0 rstd0 posb h0ced h1ed bn1 mv1 nm1 ve1 rstd1 off1 a_ined aTed aTevac qed ked ved
            qbed kbed vcopied vbed kqed scored nmaxed eed sinved attned ued qTed uTed tanhed auged
            carriedd stated0 decayedd stated1 qsed oTed
            woed h1bed bn2 mv2 ve2 rstd2 oced h2ed bn3 mv3 nm3 ve3 rstd3 off3 zed zTed zTevac zfirst
            ffned3 ffned1 gated htanh g1ed g2ed gTed gTevac downed h3ed""".split()
        names += "tabbed tabrowed pairwed pairw2ed pairTed pairTevac looked rtanhed acced".split()
        route, gate_exp, counted, table_ready, w_summed, hsummed, hsumT_pe, hsumT_act, final_pe, final_dve = (
            sem(n) for n in "route gate_exp counted table_ready w_summed hsummed hsumT_pe hsumT_act final_pe final_dve".split())
        last_in, tab_in, first8_in, first8_stored = (sem(n) for n in "last_in tab_in first8_in first8_stored".split())
        S = {n: sem("s_" + n) for n in names}

        def done(eng, name, tile, lag=0):
            value = tile[0] + 1 - lag
            if isinstance(value, int) and value < 1:
                return
            eng.wait_ge(S[name], value)

        block = ctx.enter_context(nc.Block())
        def tile_of(h, c):
            return (2 * h + c, c % 2, h + c // 2)

        def periods(eng, period, setup=None):
            tiles = lambda k: [tile_of(0, k - d) if 0 <= k - d < TILES else None for d in range(3)]
            for k in range(4):
                period(*tiles(k))
                if k == 0 and setup:
                    setup()
            with eng.Fori(2, TILES // 2) as h:
                for c in range(2):
                    period(tile_of(h, c), tile_of(h, c - 1), tile_of(h, c - 2))
            period(*tiles(TILES))
            period(*tiles(TILES + 1))

        def routed_tiles(eng, routed):
            around = lambda h, c: (tile_of(h, c - 1), tile_of(h, c), tile_of(h, c + 1))
            routed(None, *around(0, 0)[1:])
            routed(*around(0, 1))
            with eng.Fori(1, TILES // 2 - 1) as h:
                for c in range(2):
                    routed(*around(h, c))
            routed(*around(0, TILES - 2))
            routed(*around(0, TILES - 1)[:2], None)

        @block.sync
        def _(sp):
            def buffer_read(tile):
                for step in ("maxed2", "squared", "summed"):
                    done(sp, step, tile, 2)

            def load_x(tile):
                t, p, n = tile
                buffer_read(tile)
                for s in range(ST):
                    tl, bh = s // 2, s % 2
                    src = x[bh * BL:(bh + 1) * BL, bass.ds((2 * t + tl) * BLOCK, BLOCK), :]
                    sp.dma_start(xx[p][:, 0, s * JR * D:(s + 1) * JR * D],
                                 src.rearrange("b (q j) d -> b q (j d)", q=Q)).then_inc(x_in[p], 16)

            def load_last_x(tile):
                p = tile[1]
                start = (NBLK - 1) * BLOCK
                rows = ROWS - start - (Q - 1) * JR
                buffer_read(tile)
                for bh in range(2):
                    cols = xx[p][:, 0, bh * JR * D:(bh + 1) * JR * D]
                    for q in range(Q - 1):
                        sp.dma_start(cols[q:P:Q, :], x[bh * BL:(bh + 1) * BL, start + q * JR:start + (q + 1) * JR, :]
                                     .rearrange("b j d -> b (j d)")).then_inc(last_in, 16)
                    sp.dma_start(cols[Q - 1:P:Q, rows * D:], zeros[0:BL, rows * D:]).then_inc(last_in, 16)
                sp.wait_ge(last_in, 16 * 2 * Q)
                for bh in range(2):
                    sp.dma_start(xx[p][Q - 1:P:Q, 0, bh * JR * D:bh * JR * D + rows * D],
                                 x[bh * BL:(bh + 1) * BL, ROWS - rows:ROWS, :].rearrange("b j d -> b (j d)")).then_inc(x_in[p], 16)
                    sp.dma_start(xx[p][:, 0, (2 + bh) * JR * D:(3 + bh) * JR * D], zeros[:, :]).then_inc(x_in[p], 16)

            def load_pos(tile):
                t, p, n = tile
                done(sp, "posb", tile, 2)
                for tl in range(2):
                    sp.dma_start(pos[p][tl * CLIPS:(tl + 1) * CLIPS, :],
                                 a["L0_tok_pos_emb"][bass.ds(2 * t + tl, 1), :].broadcast_to([CLIPS, D])).then_inc(pos_in[p], 16)

            def store(tile, steps=2):
                t, p, n = tile
                done(sp, "h3ed", tile)
                for tl in range(steps):
                    sp.dma_start(out[:, bass.ds(2 * t + tl, 1), :].rearrange("b t d -> b (t d)"),
                                 h3[p][tl * CLIPS:(tl + 1) * CLIPS, :]).then_inc(stored[p], 16)

            sp.dma_start(const[:], a["const"]).then_inc(early_in, 16)
            sp.dma_start(wproj[:], a["L0_tok_w_proj_w"].rearrange("d a -> a d").broadcast_to([P, D])).then_inc(early_in, 16)
            sp.dma_start(wproj_b[:], a["L0_tok_w_proj_b"].rearrange("(a n) -> a n", a=1).broadcast_to([P, 1])).then_inc(early_in, 16)
            load_x(tile_of(0, 0))
            sp.dma_start(rows[:], a["rows"].broadcast_to([P, sum(ROWVECS)])).then_inc(mats_in, 16)
            sp.dma_start(mats[:], a["mats"]).then_inc(mats_in, 16)
            load_x(tile_of(0, 1))
            load_pos(tile_of(0, 0))
            for k in range(4):
                load_pos(tile_of(0, k + 1))
                load_x(tile_of(0, k + 2))
                if k >= 2:
                    store(tile_of(0, k - 2))
                if k == 2:
                    sp.dma_start(experts[:], a["experts"][:, 0:2 * E * D]).then_inc(experts_in, 16)
            with sp.Fori(2, TILES // 2 - 2) as h:
                for c in range(2):
                    load_pos(tile_of(h, c + 1))
                    load_x(tile_of(h, c + 2))
                    store(tile_of(h, c - 2))
            for k in range(TILES - 4, TILES + 2):
                if k + 1 < TILES:
                    load_pos(tile_of(0, k + 1))
                if k + 2 == TILES - 1:
                    load_last_x(tile_of(0, k + 2))
                elif k + 2 < TILES:
                    load_x(tile_of(0, k + 2))
                if k == TILES - 1:
                    for step in ("maxed2", "squared", "summed"):
                        done(sp, step, tile_of(0, k - 1))
                    sp.wait_ge(stored[0], 32 * (TILES // 2 - 1))
                    sp.wait_ge(stored[1], 32 * (TILES // 2 - 2))
                    sp.dma_start(first8[:], out[0, 0:E, :]).then_inc(first8_in, 16)
                    sp.dma_start(w2.rearrange("p e d -> p (e d)"), a["experts"][:, 2 * E * D:]).then_inc(experts_in, 16)
                if k == TILES:
                    done(sp, "tabrowed", tile_of(0, 0))
                    for s in range(2):
                        for kind in range(2):
                            sp.dma_start(tab[s * PAIRS:(s + 1) * PAIRS, kind, :],
                                         tab_rows[:, kind, :].rearrange("e (g n) -> e g n", g=E)).then_inc(tab_in, 16)
                store(tile_of(0, k - 2), 1 if k - 2 == TILES - 1 else 2)
            sp.wait_ge(stored[0], 32 * (TILES // 2))
            sp.wait_ge(stored[1], 32 * (TILES // 2) - 16)
            sp.wait_ge(final_dve, 1)
            sp.dma_start(out[0, 0:E, :], first8_out[:]).then_inc(first8_stored, 16)
            sp.wait_ge(first8_stored, 16)

        @block.gpsimd
        def _(pool):
            def rstd_of(i, tile):
                done(pool, f"mv{i}", tile)
                if i in (1, 3):
                    pool.tensor_tensor(neg_mean[i][:], mv[i][:, 0:1], const[:, C_NEG:C_NEG + 1], ALU.mult).then_inc(S[f"nm{i}"], 1)
                pool.tensor_tensor(ve[i][:], mv[i][:, 1:2], const[:, C_EPS + i:C_EPS + i + 1], ALU.add).then_inc(S[f"ve{i}"], 1)
                done(pool, f"ve{i}", tile)
                pool.tensor_tensor(rstd[i][:], ve[i][:], minus_half, ALU.pow).then_inc(S[f"rstd{i}"], 1)
                if i in (1, 3):
                    done(pool, f"nm{i}", tile)
                    done(pool, f"rstd{i}", tile)
                    pool.tensor_tensor(offset[i][:], neg_mean[i][:], rstd[i][:], ALU.mult).then_inc(S[f"off{i}"], 1)

            def products(tile, part):
                t, p, n = tile
                product = products_of[part]
                pool.wait_ge(x_in[p], 64 * (n + 1))
                done(pool, f"dot{part}", tile, 1)
                pool.tensor_tensor(product[:], xx[p][:, 0, part * JR * D:(part + 1) * JR * D].rearrange("p (j d) -> p j d", j=JR),
                                   wproj[:].rearrange("p (a d) -> p a d", a=1).broadcast_to([P, JR, D]), ALU.mult).then_inc(S[f"prod{part}"], 1)
                done(pool, f"prod{part}", tile)
                pool.tensor_tensor(product[:, :, 0], product[:, :, 0], wproj_b[:].broadcast_to([P, JR]), ALU.add).then_inc(S[f"prod{part}b"], 1)

            def carry_state(tile):
                done(pool, "stated1", tile, 1)
                done(pool, "stated0", tile, 1)
                pool.tensor_tensor(carried[:], state[1 - tile[1]][:, :, CLIPS:P], decay[:], ALU.mult).then_inc(S["carriedd"], 1)

            def spread_weights(tile):
                done(pool, "weighted", tile)
                done(pool, "summed", tile, 1)
                pool.tensor_tensor(spread[:].rearrange("p s j b -> p (s j) b"),
                                   weight[:].rearrange("p (c a) -> p c a", a=1).broadcast_to([P, ST * JR, BL]),
                                   block_mask.rearrange("p (a b) -> p a b", a=1).broadcast_to([P, ST * JR, BL]),
                                   ALU.mult).then_inc(S["spreaded"], 1)

            def add_pos(tile):
                t, p, n = tile
                pool.wait_ge(pos_in[p], 32 * (n + 1))
                done(pool, "h1ed", tile, 1)
                pool.tensor_tensor(pos_b[:], pos[p][:], ln_b, ALU.add).then_inc(S["posb"], 1)

            def key_query(tile):
                done(pool, "qbed", tile)
                done(pool, "kbed", tile)
                done(pool, "scored", tile, 1)
                pool.tensor_tensor(kb[:], qb[:], kb[:], ALU.mult).then_inc(S["kqed"], 1)

            def value_bias(tile):
                done(pool, "vcopied", tile)
                pool.tensor_tensor(vb[:], vb[:], bv, ALU.add).then_inc(S["vbed"], 1)

            def weigh_value(tile):
                done(pool, "attned", tile)
                done(pool, "vbed", tile)
                done(pool, "uTed", tile, 1)
                pool.tensor_tensor(u[:].rearrange("p (h d) -> p h d", h=HEADS), vb[:].rearrange("p (h d) -> p h d", h=HEADS),
                                   attn[:].rearrange("p (h a) -> p h a", a=1).broadcast_to([P, HEADS, HD]), ALU.mult).then_inc(S["ued"], 1)

            def add_aug(tile):
                done(pool, "qsed", tile)
                done(pool, "auged", tile)
                done(pool, "woed", tile, 2)
                pool.tensor_tensor(oT[tile[1]][:], qs[:], aug[:], ALU.add).then_inc(S["oTed"], 1)

            def residual_bias(tile):
                done(pool, "h1ed", tile)
                done(pool, "h2ed", tile, 1)
                pool.tensor_tensor(h1b[:], h1[tile[1]][:], att_b, ALU.add).then_inc(S["h1bed"], 1)

            def period(A, B, C):
                if A:
                    products(A, 2)
                    products(A, 3)
                if C:
                    residual_bias(C)
                    add_aug(C)
                if B:
                    add_pos(B)
                    rstd_of(0, B)
                    rstd_of(1, B)
                if C:
                    rstd_of(2, C)
                if A:
                    spread_weights(A)
                    if not B:
                        setup()
                if C:
                    rstd_of(3, C)
                if B:
                    key_query(B)
                    value_bias(B)
                    carry_state(B)
                    weigh_value(B)

            def table_operands():
                pool.memset(tab_diag[:], 0.0).then_inc(table_ready, 1)
                for s in range(2):
                    pool.memset(r_tanh[s][:, :, HID:HID + 1], 1.0).then_inc(table_ready, 1)
                pool.wait_ge(tab_in, 64)
                pool.tensor_tensor(tab_13[:], tab[:, 0, :], tab[:, 1, :], ALU.mult).then_inc(table_ready, 1)
                for s in range(2):
                    half = slice(s * PAIRS, (s + 1) * PAIRS)
                    pool.wait_ge(table_ready, 4 + s)
                    pool.tensor_copy(tab_diag[half, s, :], tab[half, 0, :]).then_inc(table_ready, 1)
                pool.wait_ge(table_ready, TABLE_READY)

            def squared_pairs(tile):
                t, p, n = tile
                done(pool, "acced", tile, 2)
                pool.tensor_tensor(pairs_w2[p][:],
                                   chosen_w2[:, bass.ds(2 * t, 2), :].rearrange("p s (e a) -> p s e a", a=1).broadcast_to([P, 2, E, E]),
                                   segment[:, bass.ds(2 * t, 2), :].rearrange("p s (a g) -> p s a g", a=1).broadcast_to([P, 2, E, E]),
                                   ALU.mult).then_inc(S["pairw2ed"], 1)

            def routed(before, tile, after):
                squared_pairs(tile)

            def setup():
                pool.wait_ge(setup_act, 1)
                pool.wait_ge(setup_dve, 1)
                pool.tensor_scalar(decay_cols[:], alpha_cols, 0.5, 0.5, ALU.mult, ALU.add).then_inc(setup_pool, 1)
                pool.tensor_scalar(keep_row, keep_row, -0.5, 0.5, ALU.mult, ALU.add).then_inc(setup_pool, 1)
                pool.wait_ge(setup_pool, 2)
                pool.tensor_copy(decay[:], decay_cols[:].rearrange("p (c a) -> p c a", a=1).broadcast_to([P, NC, CLIPS])).then_inc(setup_pool, 1)
                pool.tensor_tensor(bv, bv, keep_row, ALU.mult).then_inc(setup_pool, 1)
                pool.tensor_tensor(wv, wv, keep_row.rearrange("p (a n) -> p a n", a=1).broadcast_to([P, 2, CH]), ALU.mult).then_inc(setup_pool, 1)
                pool.wait_ge(setup_pool, SETUP_POOL)

            pool.wait_ge(early_in, 48)
            periods(pool, period)
            table_operands()
            pool.wait_ge(route, ROUTE_DONE)
            routed_tiles(pool, routed)

        @block.scalar
        def _(act):
            def squares(tile):
                t, p, n = tile
                act.wait_ge(x_in[p], 64 * (n + 1))
                done(act, "summed", tile, 2)
                act.activation(xx[p][:, 1, :], xx[p][:, 0, :], ACT.Square).then_inc(S["squared"], 1)

            def sum_products(tile, part):
                product = products_of[part]
                done(act, f"prod{part}b", tile)
                done(act, "shifted", tile, 1)
                for j in range(JR):
                    c = part * JR + j
                    last = act.activation(product[:, j, :], product[:, j, :], ACT.Copy, accum_out=logit[:, c:c + 1])
                last.then_inc(S[f"dot{part}"], 1)

            def exp_logits(tile):
                done(act, "shifted", tile)
                act.activation(expo[:], shifted[:], ACT.Exp).then_inc(S["exped"], 1)

            def mean_and_square(tile):
                done(act, "summed", tile)
                act.activation(mean_var[:, 0, :], bank[0][:, 0:D], ACT.Copy).then_inc(S["meaned"], 1)
                act.activation(mean_sq[:], bank[0][:, 0:D], ACT.Square).then_inc(S["msqed"], 1)

            def evacuate_stats(tile):
                p = tile[1]
                done(act, "statT", tile)
                done(act, "sprojed", tile, 2)
                act.activation(stats[p][:, 0:2, :].rearrange("p c n -> p (c n)"), bank[0][:, 0:2 * P], ACT.Copy)
                deviation = stats[p][:, 2:4, :].rearrange("p c n -> p (c n)")
                act.activation(deviation, bank[0][:, 2 * P:4 * P], ACT.Relu).then_inc(S["reluedv"], 1)
                done(act, "reluedv", tile)
                act.activation(deviation, deviation, ACT.Sqrt, bias=const[:, C_VAR:C_VAR + 1]).then_inc(S["statevac"], 1)

            def norm(i, dst, src, tile, name):
                done(act, f"off{i}", tile)
                act.activation(dst, src, ACT.Identity, bias=offset[i][:, 0:1], scale=rstd[i][:, 0:1]).then_inc(S[name], 1)

            def attention_in(tile):
                norm(1, a_in[:], h1[tile[1]][:], tile, "a_ined")

            def ffn_in(tile):
                norm(3, z[:], h2[:], tile, "zed")

            def evacuate_a(tile):
                done(act, "aTed", tile)
                act.activation(aT[:].rearrange("p c n -> p (c n)"), bank[4][:, 0:D], ACT.Copy).then_inc(S["aTevac"], 1)

            def copy_value(tile):
                done(act, "ved", tile)
                done(act, "ued", tile, 1)
                act.activation(vb[:], bank[4][:, :], ACT.Copy).then_inc(S["vcopied"], 1)

            def exp_scores(tile):
                done(act, "nmaxed", tile)
                act.activation(e_score[:], score[:], ACT.Exp, bias=neg_max[:, 0:1], accum_out=s_sum[:, 0:1]).then_inc(S["eed"], 1)

            def augment_tanh(tile):
                done(act, "qTed", tile)
                done(act, "oTed", tile, 1)
                for c in range(NC):
                    last = act.activation(aug[:, c, :], bank[5][:, c * P:(c + 1) * P], ACT.Tanh, scale=aug_cols[:, c:c + 1])
                last.then_inc(S["tanhed"], 1)

            def augment(tile):
                done(act, "tanhed", tile)
                act.activation(aug[:], aug[:], ACT.Copy, bias=0.5, scale=0.5).then_inc(S["auged"], 1)

            def evacuate_z(tile):
                t = tile[0]
                done(act, "zTed", tile)
                act.activation(zT[:].rearrange("p c n -> p (c n)"), bank[7][:, 0:D], ACT.Copy).then_inc(S["zTevac"], 1)
                act.activation(z_first[:, :, bass.ds(2 * t, 2)], bank[7][:, 0:D].rearrange("p (c n) -> p c n", c=2)[:, :, 0:P:CLIPS],
                               ACT.Copy).then_inc(S["zfirst"], 1)

            def gate_and_tanh(tile):
                t = tile[0]
                done(act, "ffned1", tile)
                act.activation(gate[:, bass.ds(t, 1), :].rearrange("p a e -> p (a e)"), bank[6][:, 0:E], ACT.Copy).then_inc(S["gated"], 1)
                done(act, "g1ed", tile, 1)
                act.activation(half_tanh[:], bank[6][:, E:E + D], ACT.Tanh, scale=0.5).then_inc(S["htanh"], 1)

            def evacuate_g(tile):
                done(act, "gTed", tile)
                act.activation(gT[:].rearrange("p c n -> p (c n)"), bank[6][:, 0:D], ACT.Copy).then_inc(S["gTevac"], 1)

            def period(A, B, C):
                if A:
                    sum_products(A, 2)
                    sum_products(A, 3)
                    exp_logits(A)
                if B:
                    if not A:
                        exp_gates(0, 0, EARLY)
                    attention_in(B)
                    evacuate_a(B)
                if A:
                    squares(A)
                    if not B:
                        setup()
                if C:
                    ffn_in(C)
                if B:
                    copy_value(B)
                if C:
                    evacuate_z(C)
                if B:
                    exp_scores(B)
                if A:
                    mean_and_square(A)
                if C:
                    gate_and_tanh(C)
                    if not A and not B:
                        exp_gates(1, EARLY, TILES)
                        table_rows()
                if B:
                    augment_tanh(B)
                if C:
                    evacuate_g(C)
                if A:
                    evacuate_stats(A)
                if B:
                    augment(B)

            def exp_gates(batch, lo, hi):
                act.wait_ge(route, GATE_SHIFTED[batch])
                act.activation(sc[:, lo:hi, :], sc[:, lo:hi, :], ACT.Exp).then_inc(gate_exp, 1)

            def table_rows():
                done(act, "tabbed", tile_of(0, 0))
                for b in range(4):
                    last = act.activation(tab_rows[:, b // 2, (b % 2) * 512:(b % 2 + 1) * 512], bank[b][0:E, :], ACT.Copy)
                last.then_inc(S["tabrowed"], 1)

            def routed(before, tile, after):
                p = tile[1]
                done(act, "looked", tile)
                done(act, "acced", tile, 2)
                act.activation(r_tanh[p][:, :, 0:HID], bank[4 + p][:, 0:2 * HID].rearrange("p (s n) -> p s n", s=2),
                               ACT.Tanh, scale=0.5).then_inc(S["rtanhed"], 1)

            def setup():
                act.wait_ge(mats_in, 32)
                act.activation(alpha_cols, alpha_cols, ACT.Tanh, scale=0.5)
                act.activation(keep_row, keep_row, ACT.Tanh, scale=0.5).then_inc(setup_act, 1)
                act.activation(aug_cols, aug_cols, ACT.Copy, scale=0.5)
                act.activation(bk, bk, ACT.Copy, scale=HD ** -0.5)
                act.activation(wk, wk, ACT.Copy, scale=HD ** -0.5).then_inc(setup_act, 1)
                act.wait_ge(setup_act, 2)

            act.wait_ge(early_in, 48)
            periods(act, period)
            act.wait_ge(table_ready, TABLE_READY)
            routed_tiles(act, routed)
            act.wait_ge(hsumT_pe, 1)
            act.activation(hsumT[:], bank[1][:, 0:PAIRS], ACT.Copy, scale=0.5).then_inc(hsumT_act, 1)

        @block.tensor
        def _(pe):
            def logit_max_rows(tile):
                done(pe, "lmaxed", tile)
                pe.transpose(bank[1][0:ST, 0:P], logit_max[:], ident).then_inc(S["lmaxT"], 1)

            def block_max_cols(tile):
                done(pe, "bmaxed", tile)
                pe.matmul(bank[1][:, P:P + ST], block_max4[:].rearrange("s b q -> s (b q)"),
                          ident[0:ST, 0:ST], start=True, stop=True).then_inc(S["bmaxT"], 1)

            def block_sums(tile):
                done(pe, "esummed", tile)
                pe.matmul(bank[1][:, P:P + ST], same_block, expo_sum[:], start=True, stop=True).then_inc(S["denned"], 1)

            def weighted_sums(tile):
                p = tile[1]
                done(pe, "spreaded", tile)
                done(pe, "squared", tile)
                done(pe, "statevac", tile, 1)
                for j in range(JR):
                    for s in range(ST):
                        col = (s * JR + j) * D
                        last = pe.matmul(bank[0][s * BL:(s + 1) * BL, :], spread[:, s, j, :], xx[p][:, :, col:col + D],
                                         start=(j == 0), stop=(j == JR - 1), tile_position=(0, s * BL))
                last.then_inc(S["summed"], 1)

            def transpose_maxima(tile):
                done(pe, "maxed1", tile)
                done(pe, "maxq", tile, 1)
                for c in range(2):
                    for s in range(ST):
                        last = pe.transpose(bank[2 + c][:, s * P:(s + 1) * P], max1[:, s, c * P:(c + 1) * P], ident)
                last.then_inc(S["maxT"], 1)

            def transpose_stats(tile):
                done(pe, "varred", tile)
                for c in range(4):
                    last = pe.transpose(bank[0][:, c * P:(c + 1) * P], mean_var[:, c // 2, (c % 2) * P:(c % 2 + 1) * P], ident)
                last.then_inc(S["statT"], 1)

            def project_stats(tile):
                p = tile[1]
                done(pe, "statevac", tile)
                done(pe, "maxq", tile)
                done(pe, "stated1", tile, 1)
                for c in range(6):
                    last = pe.matmul(bank[4][:, 0:D], stats[p][:, c, :], sproj[:, c, :], start=(c == 0), stop=False)
                last = pe.matmul(bank[4][:, 0:D], ones[0:1, :], sproj_b[0:1, :], start=False, stop=True)
                last.then_inc(S["sprojed"], 1)

            def transpose_a(tile):
                done(pe, "a_ined", tile)
                for c in range(2):
                    last = pe.transpose(bank[4][:, c * P:(c + 1) * P], a_in[:, c * P:(c + 1) * P], ident)
                last.then_inc(S["aTed"], 1)

            def linear(to, w):
                for c in range(2):
                    last = pe.matmul(to, aT[:, c, :], w[:, c, :], start=(c == 0), stop=(c == 1))
                return last

            def query(tile):
                done(pe, "aTevac", tile)
                linear(bank[4][:, :], wq).then_inc(S["qed"], 1)

            def key(tile):
                done(pe, "aTevac", tile)
                done(pe, "qsed", tile, 1)
                linear(bank[5][:, :], wk).then_inc(S["ked"], 1)

            def value(tile):
                done(pe, "qbed", tile)
                linear(bank[4][:, :], wv).then_inc(S["ved"], 1)

            def transpose_q(tile):
                done(pe, "kbed", tile)
                for c in range(NC):
                    last = pe.transpose(bank[5][:, c * P:(c + 1) * P], qb[:, c * P:(c + 1) * P], ident)
                last.then_inc(S["qTed"], 1)

            def transpose_u(tile):
                done(pe, "ued", tile)
                for c in range(NC):
                    last = pe.transpose(bank[4][:, c * P:(c + 1) * P], u[:, c * P:(c + 1) * P], ident)
                last.then_inc(S["uTed"], 1)

            def project_out(tile):
                p = tile[1]
                done(pe, "oTed", tile)
                done(pe, "gTevac", tile, 1)
                for c in range(NC):
                    last = pe.matmul(bank[6][:, 0:D], oT[p][:, c, :], wo[:, c, :], start=(c == 0), stop=False)
                last = pe.matmul(bank[6][:, 0:D], ones[0:1, :], bo[0:1, :], start=False, stop=True)
                last.then_inc(S["woed"], 1)

            def transpose_z(tile):
                done(pe, "zed", tile)
                done(pe, "h3ed", tile, 1)
                for c in range(2):
                    last = pe.transpose(bank[7][:, c * P:(c + 1) * P], z[:, c * P:(c + 1) * P], ident)
                last.then_inc(S["zTed"], 1)

            def ffn_up1(tile):
                done(pe, "zTevac", tile)
                for c in range(2):
                    last = pe.matmul(bank[6][:, 0:E + D], zT[:, c, :], gate_up1[:, c, :], start=(c == 0), stop=(c == 1))
                last.then_inc(S["ffned1"], 1)

            def ffn_up3(tile):
                done(pe, "zfirst", tile)
                for c in range(2):
                    last = pe.matmul(bank[7][:, 0:D], zT[:, c, :], up3[:, c, :], start=(c == 0), stop=(c == 1))
                last.then_inc(S["ffned3"], 1)

            def transpose_g(tile):
                done(pe, "g2ed", tile)
                for c in range(2):
                    last = pe.transpose(bank[6][:, c * P:(c + 1) * P], g2[:, c * P:(c + 1) * P], ident)
                last.then_inc(S["gTed"], 1)

            def ffn_down(tile):
                done(pe, "gTevac", tile)
                for c in range(2):
                    last = pe.matmul(bank[7][:, 0:D], gT[:, c, :], down[:, c, :], start=(c == 0), stop=(c == 1))
                last.then_inc(S["downed"], 1)

            def hold_clock(n):
                for _ in range(n):
                    pe.matmul(bank[0][:, 0:D], ident, const[:, 0:D], start=True, stop=True)

            def period(A, B, C):
                if B:
                    project_stats(B)
                    hold_clock(2)
                if A:
                    logit_max_rows(A)
                    hold_clock(2)
                    block_max_cols(A)
                if C:
                    project_out(C)
                    if not A and not B:
                        table(3)
                    elif not A:
                        table(0)
                if B:
                    transpose_a(B)
                if A:
                    block_sums(A)
                if B:
                    query(B)
                    key(B)
                    value(B)
                if C:
                    transpose_z(C)
                if A:
                    weighted_sums(A)
                if C:
                    ffn_up1(C)
                    ffn_up3(C)
                if B:
                    transpose_q(B)
                    transpose_u(B)
                if A:
                    transpose_stats(A)
                if C:
                    transpose_g(C)
                if A:
                    transpose_maxima(A)
                if C:
                    ffn_down(C)
                    if B and not A:
                        table(1)
                        table(2)

            def table(b):
                if b == 0:
                    pe.wait_ge(experts_in, 16)
                    done(pe, "zfirst", tile_of(0, E // 2 - 1))
                w = (w1, w3)[b // 2]
                for c in range(2):
                    last = pe.matmul(bank[b][0:E, :], z_first[:, c, 0:E], w[:, c, (b % 2) * 4:(b % 2 + 1) * 4, :],
                                     start=(c == 0), stop=(c == 1))
                if b == 3:
                    last.then_inc(S["tabbed"], 1)

            def transpose_pairs(tile):
                p = tile[1]
                done(pe, "pairwed", tile)
                done(pe, "pairTevac", tile, 2)
                pe.transpose(bank[1 + p][:, 0:P], pairs_w[p][:].rearrange("p s e g -> p (s e g)"), ident).then_inc(S["pairTed"], 1)

            def look_up(tile):
                p = tile[1]
                done(pe, "pairTevac", tile)
                done(pe, "rtanhed", tile, 2)
                pe.matmul(bank[4 + p][:, 0:2 * HID], pairs_wT[p][:], tab_diag[:].rearrange("p s n -> p (s n)"),
                          start=True, stop=True).then_inc(S["looked"], 1)

            def accumulate(tile, first=False):
                p = tile[1]
                done(pe, "rtanhed", tile)
                done(pe, "pairw2ed", tile)
                for s in range(2):
                    last = pe.matmul(bank[0][s * PAIRS:(s + 1) * PAIRS, 0:HID + 1], pairs_w2[p][:, s].rearrange("p e g -> p (e g)"),
                                     r_tanh[p][:, s, :], start=first, stop=True, skip_group_check=True)
                last.then_inc(S["acced"], 1)

            def routed(before, tile, after):
                if after:
                    transpose_pairs(after)
                look_up(tile)
                if before:
                    accumulate(before, first=isinstance(before[0], int) and before[0] == 0)

            def setup():
                pe.wait_ge(mats_in, 32)
                pe.wait_ge(setup_act, 2)
                pe.wait_ge(setup_pool, SETUP_POOL)

            pe.wait_ge(early_in, 48)
            periods(pe, period, setup)
            pe.wait_ge(route, COUNT_READY)
            pe.matmul(bank[3][:, 0:E], ones, mine[:], start=True, stop=True).then_inc(counted, 1)
            pe.wait_ge(table_ready, TABLE_READY)
            done(pe, "tabrowed", tile_of(0, 0))
            transpose_pairs(tile_of(0, 0))
            routed_tiles(pe, routed)
            accumulate(tile_of(0, TILES - 1))
            pe.wait_ge(hsummed, 1)
            pe.matmul(bank[1][:, 0:PAIRS], hsum[:], const[:, C_SEL:C_SEL + PAIRS], start=True, stop=True).then_inc(hsumT_pe, 1)
            pe.wait_ge(experts_in, 32)
            pe.wait_ge(hsumT_act, 1)
            for g in range(E):
                last = pe.matmul(bank[3][0:E, 0:D], hsumT[:, g:PAIRS:E], w2[:, g, :], start=(g == 0), stop=(g == E - 1))
            last.then_inc(final_pe, 1)

        @block.vector
        def _(dve):
            def dots(tile, part):
                t, p, n = tile
                if part == 0:
                    dve.wait_ge(x_in[p], 64 * (n + 1))
                done(dve, f"dot{1 - part}", tile, 1 - part)
                for c in range(part * JR, (part + 1) * JR):
                    last = dve.tensor_tensor_reduce(out=product[:, c % JR, :], in0=xx[p][:, 0, c * D:(c + 1) * D], in1=wproj[:],
                                                    scale=1.0, scalar=wproj_b[:, 0:1], op0=ALU.mult, op1=ALU.add,
                                                    accum_out=logit[:, c:c + 1])
                last.then_inc(S[f"dot{part}"], 1)

            def maxima2(tile):
                p = tile[1]
                dve.wait_ge(x_in[p], 64 * (tile[2] + 1))
                rows = xx[p][:, 0, :].rearrange("p (s n) -> p s n", s=ST)
                dve.tensor_tensor(max2[:], rows[:, :, 0:2 * D], rows[:, :, 2 * D:4 * D], ALU.max).then_inc(S["maxed2"], 1)

            def maxima1(tile):
                done(dve, "maxed2", tile)
                done(dve, "maxT", tile, 1)
                dve.tensor_tensor(max1[:], max2[:, :, 0:D], max2[:, :, D:2 * D], ALU.max).then_inc(S["maxed1"], 1)

            def maxima_of_blocks(tile):
                done(dve, "maxT", tile)
                done(dve, "sprojed", tile, 2)
                dve.tensor_reduce(stats[tile[1]][:, 4:6, :], psum[:, 2:4, :].rearrange("p c (n q) -> p c n q", q=Q),
                                  AX.X, ALU.max).then_inc(S["maxq"], 1)

            def logit_max_of_rows(tile):
                for part in range(1, ST):
                    done(dve, f"dot{part}", tile)
                dve.tensor_reduce(logit_max[:], logit[:].rearrange("p (s j) -> p s j", j=JR), AX.X, ALU.max).then_inc(S["lmaxed"], 1)

            def logit_max_of_blocks(tile):
                done(dve, "lmaxT", tile)
                dve.tensor_reduce(block_max[:], bank[1][0:ST, 0:P].rearrange("s (b q) -> s b q", q=Q), AX.X, ALU.max).then_inc(S["bmaxed0"], 1)
                done(dve, "bmaxed0", tile)
                dve.tensor_copy(block_max4[:], block_max[:].rearrange("s (b a) -> s b a", a=1).broadcast_to([ST, BL, Q])).then_inc(S["bmaxed"], 1)

            def per_block(ap):
                return ap.rearrange("p (s a) -> p s a", a=1).broadcast_to([P, ST, JR])

            def shift_logits(tile):
                done(dve, "bmaxT", tile)
                dve.tensor_tensor(shifted[:].rearrange("p (s j) -> p s j", j=JR), logit[:].rearrange("p (s j) -> p s j", j=JR),
                                  per_block(bank[1][:, P:P + ST]), ALU.subtract).then_inc(S["shifted"], 1)

            def sum_expo(tile):
                done(dve, "exped", tile)
                dve.tensor_reduce(expo_sum[:], expo[:].rearrange("p (s j) -> p s j", j=JR), AX.X, ALU.add).then_inc(S["esummed"], 1)

            def normalise(tile):
                done(dve, "denned", tile)
                dve.reciprocal(inv_sum[:], bank[1][:, P:P + ST]).then_inc(S["rdenned"], 1)
                done(dve, "rdenned", tile)
                dve.tensor_tensor(weight[:].rearrange("p (s j) -> p s j", j=JR), expo[:].rearrange("p (s j) -> p s j", j=JR),
                                  per_block(inv_sum[:]), ALU.mult).then_inc(S["weighted"], 1)

            def variance(tile):
                done(dve, "msqed", tile)
                dve.tensor_tensor(mean_var[:, 1, :], bank[0][:, D:2 * D], mean_sq[:], ALU.subtract).then_inc(S["varred"], 1)

            def norm_stats(i, src, tile, ready):
                done(dve, ready, tile)
                dve.bn_stats(bn[i][:], src).then_inc(S[f"bn{i}"], 1)
                done(dve, f"bn{i}", tile)

            def norm_mean(i, tile):
                dve.bn_aggr(mv[i][:], bn[i][:]).then_inc(S[f"mv{i}"], 1)

            def token(tile):
                norm_stats(0, bank[4][:, 0:D], tile, "sprojed")

            def token_scale(tile):
                done(dve, "mv0", tile)
                done(dve, "h1ed", tile, 1)
                dve.scalar_tensor_tensor(out=h0[:], in0=bank[4][:, 0:D], scalar=mv[0][:, 0:1], in1=ln_g, op0=ALU.subtract, op1=ALU.mult).then_inc(S["h0ced"], 1)

            def token_out(tile):
                p = tile[1]
                done(dve, "rstd0", tile)
                done(dve, "posb", tile)
                done(dve, "h0ced", tile)
                done(dve, "h1bed", tile, 2)
                dve.scalar_tensor_tensor(out=h1[p][:], in0=h0[:], scalar=rstd[0][:, 0:1], in1=pos_b[:], op0=ALU.mult, op1=ALU.add).then_inc(S["h1ed"], 1)
                norm_stats(1, h1[p][:], tile, "h1ed")

            def query_bias(tile):
                done(dve, "qed", tile)
                done(dve, "qTed", tile, 1)
                done(dve, "kqed", tile, 1)
                dve.tensor_tensor(qb[:], bank[4][:, :], bq, ALU.add).then_inc(S["qbed"], 1)

            def key_bias(tile):
                done(dve, "scored", tile, 1)
                done(dve, "ked", tile)
                dve.tensor_tensor(kb[:], bank[5][:, :], bk, ALU.add).then_inc(S["kbed"], 1)

            def scores(tile):
                done(dve, "kqed", tile)
                dve.tensor_reduce(score[:], kb[:].rearrange("p (h d) -> p h d", h=HEADS), AX.X, ALU.add).then_inc(S["scored"], 1)
                done(dve, "scored", tile)
                dve.tensor_reduce(neg_max[:], score[:], AX.X, ALU.max, negate=True).then_inc(S["nmaxed"], 1)

            def head_softmax(tile):
                done(dve, "eed", tile)
                dve.reciprocal(s_inv[:], s_sum[:]).then_inc(S["sinved"], 1)
                done(dve, "sinved", tile)
                dve.tensor_scalar(attn[:], e_score[:], s_inv[:, 0:1], None, ALU.mult).then_inc(S["attned"], 1)

            def advance_state(tile):
                now, u_now = state[tile[1]], bank[4][:, :].rearrange("p (c n) -> p c n", c=NC)
                done(dve, "uTed", tile)
                done(dve, "carriedd", tile)
                dve.tensor_tensor(now[:, :, 0:CLIPS], carried[:], u_now[:, :, 0:CLIPS], ALU.add).then_inc(S["stated0"], 1)
                done(dve, "stated0", tile)
                dve.tensor_tensor(decayed[:], now[:, :, 0:CLIPS], decay[:], ALU.mult).then_inc(S["decayedd"], 1)
                done(dve, "decayedd", tile)
                dve.tensor_tensor(now[:, :, CLIPS:P], decayed[:], u_now[:, :, CLIPS:P], ALU.add).then_inc(S["stated1"], 1)

            def query_state(tile):
                done(dve, "stated1", tile)
                done(dve, "tanhed", tile)
                done(dve, "oTed", tile, 1)
                dve.tensor_tensor(qs[:], bank[5][:, :].rearrange("p (c n) -> p c n", c=NC), state[tile[1]][:], ALU.mult).then_inc(S["qsed"], 1)

            def attention_out(tile):
                norm_stats(2, bank[6][:, 0:D], tile, "woed")

            def attention_scale(tile):
                done(dve, "mv2", tile)
                done(dve, "h2ed", tile, 1)
                dve.scalar_tensor_tensor(out=o_raw[:], in0=bank[6][:, 0:D], scalar=mv[2][:, 0:1], in1=att_g, op0=ALU.subtract, op1=ALU.mult).then_inc(S["oced"], 1)

            def residual(tile):
                done(dve, "rstd2", tile)
                done(dve, "h1bed", tile)
                done(dve, "oced", tile)
                dve.scalar_tensor_tensor(out=h2[:], in0=o_raw[:], scalar=rstd[2][:, 0:1], in1=h1b[:], op0=ALU.mult, op1=ALU.add).then_inc(S["h2ed"], 1)
                norm_stats(3, h2[:], tile, "h2ed")

            def silu_a(tile):
                done(dve, "htanh", tile)
                dve.scalar_tensor_tensor(out=half_tanh[:], in0=half_tanh[:], scalar=1.0, in1=bank[6][:, E:E + D], op0=ALU.add, op1=ALU.mult).then_inc(S["g1ed"], 1)

            def silu_b(tile):
                done(dve, "ffned3", tile)
                done(dve, "g1ed", tile)
                dve.scalar_tensor_tensor(out=g2[:], in0=half_tanh[:], scalar=0.5, in1=bank[7][:, 0:D], op0=ALU.mult, op1=ALU.mult).then_inc(S["g2ed"], 1)

            def result(tile):
                t, p, n = tile
                done(dve, "downed", tile)
                if not (isinstance(n, int) and n < 1):
                    dve.wait_ge(stored[p], 32 * n)
                dve.tensor_tensor(h3[p][:], bank[7][:, 0:D], h2[:], ALU.add).then_inc(S["h3ed"], 1)

            def period(A, B, C):
                if A:
                    dots(A, 0)
                    dots(A, 1)
                if B:
                    if not A:
                        route_scores(0, 0, EARLY)
                    token(B)
                if A:
                    logit_max_of_rows(A)
                if B:
                    norm_mean(0, B)
                    token_scale(B)
                if A:
                    logit_max_of_blocks(A)
                if B:
                    token_out(B)
                if A:
                    shift_logits(A)
                if B:
                    norm_mean(1, B)
                if C:
                    attention_out(C)
                if A:
                    sum_expo(A)
                if C:
                    norm_mean(2, C)
                    attention_scale(C)
                    residual(C)
                    if B and not A:
                        route_groups(0, EARLY)
                if A:
                    normalise(A)
                if C:
                    norm_mean(3, C)
                if B:
                    query_bias(B)
                    key_bias(B)
                    if not A:
                        route_expert(0, 0, EARLY)
                if A:
                    maxima2(A)
                if B:
                    scores(B)
                    head_softmax(B)
                if A:
                    maxima1(A)
                    variance(A)
                if C:
                    if not B:
                        route_scores(1, EARLY, TILES)
                    silu_a(C)
                    if not B:
                        route_groups(EARLY, TILES)
                    silu_b(C)
                    if not B:
                        for slot in range(2):
                            route_expert(slot, EARLY, TILES)
                if B:
                    advance_state(B)
                    query_state(B)
                if A:
                    maxima_of_blocks(A)
                if C:
                    result(C)
                    if B and not A:
                        route_expert(1, 0, EARLY)
                        route_weights(0, EARLY)

            steps = [0]

            def link(instruction):
                steps[0] += 1
                instruction.then_inc(route, 1)
                dve.wait_ge(route, steps[0])

            def cols(ap, n):
                return ap.rearrange("p (t a) -> p t a", a=1).broadcast_to([P, ap.shape[1], n])

            def route_scores(batch, lo, hi):
                n = hi - lo
                done(dve, "gated", tile_of(0, hi - 1))
                link(dve.tensor_reduce(t1[:, lo:hi], gate[:, lo:hi, :], AX.X, ALU.max))
                link(dve.tensor_tensor(sc[:, lo:hi, :], gate[:, lo:hi, :], cols(t1[:, lo:hi], E), ALU.subtract))
                assert steps[0] == GATE_SHIFTED[batch], steps
                dve.wait_ge(gate_exp, batch + 1)
                link(dve.tensor_reduce(t1[:, lo:hi], sc[:, lo:hi, :], AX.X, ALU.add))
                link(dve.reciprocal(t1[:, lo:hi], t1[:, lo:hi]))
                link(dve.tensor_tensor(sc[:, lo:hi, :], sc[:, lo:hi, :], cols(t1[:, lo:hi], E), ALU.mult))
                link(dve.tensor_tensor(s2[:, lo:hi, :], sc[:, lo:hi, :],
                                       ebias.rearrange("p (a e) -> p a e", a=1).broadcast_to([P, n, E]), ALU.add))
                link(dve.tensor_reduce(gsum[:, lo:hi, :], s2[:, lo:hi, :].rearrange("p t (g m) -> p t g m", m=E // G), AX.X, ALU.add))

            def route_groups(lo, hi):
                n = hi - lo
                gt, ge, rank, values = cmp_gt[:, lo:hi], cmp_ge[:, lo:hi], grank[:, lo:hi, :], gsum[:, lo:hi, :]
                other = values.rearrange("p t (a b) -> p t a b", a=1).broadcast_to([P, n, G, G])
                own = values.rearrange("p t (a b) -> p t a b", b=1).broadcast_to([P, n, G, G])
                before = const[:, C_LT4:C_LT4 + G * G].rearrange("p (z a b) -> p z a b", z=1, a=G).broadcast_to([P, n, G, G])
                dve.tensor_tensor(gt, other, own, ALU.is_gt)
                link(dve.tensor_tensor(ge, other, own, ALU.is_ge))
                link(dve.tensor_tensor(ge, ge, before, ALU.mult))
                link(dve.tensor_tensor(gt, gt, ge, ALU.max))
                link(dve.tensor_reduce(rank, gt, AX.X, ALU.add))
                link(dve.tensor_scalar(rank, rank, 2.0, -1e30, ALU.is_ge, ALU.mult))
                by_group = s2[:, lo:hi, :].rearrange("p t (g m) -> p t g m", m=E // G)
                link(dve.tensor_tensor(by_group, by_group, rank.rearrange("p t (g a) -> p t g a", a=1).broadcast_to([P, n, G, E // G]), ALU.add))

            def route_expert(slot, lo, hi):
                n = hi - lo
                s2_, equal_, best_ = s2[:, lo:hi, :], equal[:, lo:hi, :], best[:, lo:hi]
                by_slot = chosen[:].rearrange("p (t s) e -> p t s e", s=2)
                if slot > 0:
                    link(dve.scalar_tensor_tensor(out=s2_, in0=by_slot[:, lo:hi, slot - 1, :], scalar=-2e30, in1=s2_,
                                                  op0=ALU.mult, op1=ALU.add))
                link(dve.tensor_reduce(best_, s2_, AX.X, ALU.max))
                link(dve.tensor_tensor(equal_, s2_, cols(best_, E), ALU.is_ge))
                link(dve.tensor_tensor(equal_, equal_, const[:, C_DESC:C_DESC + E].rearrange("p (a e) -> p a e", a=1).broadcast_to([P, n, E]),
                                       ALU.mult))
                link(dve.tensor_reduce(best_, equal_, AX.X, ALU.max))
                link(dve.tensor_tensor(by_slot[:, lo:hi, slot, :], equal_, cols(best_, E), ALU.is_ge))

            def route_weights(lo, hi):
                both = lambda ap: ap[:].rearrange("p (t s) e -> p t s e", s=2)[:, lo:hi]
                for s in range(2):
                    last = dve.tensor_tensor(both(chosen_w)[:, :, s, :], both(chosen)[:, :, s, :], sc[:, lo:hi, :], ALU.mult)
                link(last)
                entries = slice(2 * lo, 2 * hi)
                link(dve.tensor_tensor(chosen_w2[:, entries, :], chosen_w[:, entries, :], chosen_w[:, entries, :], ALU.mult))

            def weigh_pairs(tile):
                t, p, n = tile
                done(dve, "pairTed", tile, 2)
                dve.tensor_tensor(pairs_w[p][:],
                                  chosen_w[:, bass.ds(2 * t, 2), :].rearrange("p s (e a) -> p s e a", a=1).broadcast_to([P, 2, E, E]),
                                  segment[:, bass.ds(2 * t, 2), :].rearrange("p s (a g) -> p s a g", a=1).broadcast_to([P, 2, E, E]),
                                  ALU.mult).then_inc(S["pairwed"], 1)

            def evacuate_pairs(tile):
                p = tile[1]
                done(dve, "pairTed", tile)
                done(dve, "looked", tile, 2)
                dve.tensor_copy(pairs_wT[p][:], bank[1 + p][:, 0:P]).then_inc(S["pairTevac"], 1)

            def routed(before, tile, after):
                if after:
                    weigh_pairs(after)
                evacuate_pairs(tile)

            def setup():
                dve.wait_ge(mats_in, 32)
                dve.wait_ge(setup_act, 2)
                dve.wait_ge(setup_pool, SETUP_POOL)

            dve.memset(state[1][:], 0.0).then_inc(setup_dve, 1)
            dve.wait_ge(early_in, 48)
            periods(dve, period, setup)

            link(dve.memset(chosen[CLIPS:P, 2 * TILES - 2:2 * TILES, :], 0.0))
            link(dve.tensor_reduce(mine[:], chosen[:].rearrange("p n e -> p e n"), AX.X, ALU.add))
            assert steps[0] == COUNT_READY, steps
            route_weights(EARLY, TILES)
            dve.wait_ge(counted, 1)
            link(dve.tensor_copy(count[:], bank[3][:, 0:E]))
            link(dve.tensor_tensor_scan(seg_end[:], ones[:, 0:E], count[:], 0.0, ALU.mult, ALU.add))
            link(dve.tensor_tensor(seg_start[:], seg_end[:], count[:], ALU.subtract))
            position = const[:, C_POS:C_POS + 2 * TILES].rearrange("p (n a) -> p n a", a=1).broadcast_to([P, 2 * TILES, E])
            bounds = lambda ap: ap.rearrange("p (a e) -> p a e", a=1).broadcast_to([P, 2 * TILES, E])
            dve.tensor_tensor(segment[:], position, bounds(seg_start[:]), ALU.is_ge)
            link(dve.tensor_tensor(seg_hi[:], position, bounds(seg_end[:]), ALU.is_lt))
            link(dve.tensor_tensor(segment[:], segment[:], seg_hi[:], ALU.mult))
            assert steps[0] == ROUTE_DONE, steps
            weigh_pairs(tile_of(0, 0))
            routed_tiles(dve, routed)
            done(dve, "acced", tile_of(0, TILES - 1))
            dve.tensor_copy(w_sum[:], bank[0][:, HID:HID + 1]).then_inc(w_summed, 1)
            dve.wait_ge(table_ready, TABLE_READY)
            dve.wait_ge(w_summed, 1)
            dve.scalar_tensor_tensor(out=hsum[:], in0=bank[0][:, 0:HID], scalar=w_sum[:, 0:1], in1=tab_13[:],
                                     op0=ALU.add, op1=ALU.mult).then_inc(hsummed, 1)
            dve.wait_ge(final_pe, 1)
            dve.wait_ge(first8_in, 16)
            dve.tensor_tensor(first8_out[:], bank[3][0:E, 0:D], first8[:], ALU.add).then_inc(final_dve, 1)


SETUP_POOL = 5
TABLE_READY = 6
EARLY = TILES - 2
GATE_SHIFTED, COUNT_READY, ROUTE_DONE = (2, 28), 52, 59

SHAPE = (CLIPS, NBLK, D)


def kernel(**inputs):
    import concourse.bacc as bacc
    from concourse.bass_utils import run_bass_kernel_spmd

    arrays = {n: np.ascontiguousarray(v) for n, v in inputs.items()}
    on_partitions = lambda w: w.reshape(-1, P, w.shape[-1]).transpose(1, 0, 2).reshape(P, -1)
    take = arrays.pop
    sw1, sw2, sw3 = (take("L0_ffn_" + n).T for n in ("sw1", "sw2", "sw3"))
    gate_sw1 = np.concatenate([take("L0_ffn_w_gate").T, sw1], axis=1)
    columns = lambda v: v.reshape(NC, P).T
    arrays["mats"] = np.concatenate(
        [on_partitions(w) for w in (take("L0_tok_s_proj_w"), take("L0_attn_Wq"), take("L0_attn_Wk"), take("L0_attn_Wv"), take("L0_attn_Wo"),
                                    gate_sw1, sw3, sw2)]
        + [columns(arrays["L0_attn_alpha"]), columns(take("L0_attn_aug_param"))], axis=1)
    arrays["rows"] = np.concatenate([take(n).reshape(1, -1) for n in (
        "L0_tok_s_proj_b", "L0_tok_ln_g", "L0_tok_ln_b", "L0_attn_bo", "L0_attn_ln_scale", "L0_attn_ln_bias",
        "L0_attn_bq", "L0_attn_bk", "L0_attn_bv", "L0_attn_alpha", "L0_ffn_expert_bias")], axis=1)
    arrays["experts"] = np.concatenate(
        [take("L0_ffn_" + n).reshape(E, 2, P, HID).transpose(2, 1, 0, 3).reshape(P, -1) for n in ("w1", "w3")]
        + [take("L0_ffn_w2").transpose(1, 0, 2).reshape(P, -1)], axis=1)
    arrays["const"] = constants()
    arrays["zeros"] = np.zeros((P, JR * D), np.float32)
    nc = bacc.Bacc("TRN2", target_bir_lowering=False, num_devices=1)
    aps = {n: nc.dram_tensor("in_" + n, v.shape, mybir.dt.from_np(v.dtype), kind="ExternalInput").ap() for n, v in arrays.items()}
    out = nc.dram_tensor("tower_out", SHAPE, F32, kind="ExternalOutput").ap()
    audio_tower(nc, aps, out)
    r = run_bass_kernel_spmd(nc, [{"in_" + n: v for n, v in arrays.items()}], core_ids=[0])
    return r.results[0]["tower_out"]
```
